# Optimizing a Trainium2 kernel written in Bass

```python
import numpy as np
import jax
import jax.numpy as jnp

def _softmax(x, axis=-1):
    return jax.nn.softmax(x, axis=axis)

def _gelu(x):
    return jax.nn.gelu(x, approximate=True)

def _silu(x):
    return jax.nn.silu(x)

def _sigmoid(x):
    return jax.nn.sigmoid(x)

def _layernorm(x, axis=-1, eps=1e-05):
    m = jnp.mean(x, axis=axis, keepdims=True)
    v = jnp.var(x, axis=axis, keepdims=True)
    return (x - m) / jnp.sqrt(v + eps)

def _scatter_add(tgt, idx, src, axis=0):
    return tgt.at[idx].add(src)

def _segment_sum(src, seg, n):
    return jax.ops.segment_sum(src, seg, n)
kernel_name = 'mk_prb_d1_jaxref_r4_fc8c6e'

def setup_inputs(seed: int=0):
    np.random.seed(seed)
    _w = jnp.asarray

    def _L0_attn_setup():
        import jax, jax.numpy as jnp
        import numpy as np
        H = 16
        D_IN = 512
        D_H = D_IN // H
        key = jax.random.key(seed)
        k1, k2, k3 = jax.random.split(key, 3)
        b, L = (2, 512)
        x = jax.random.normal(k1, (b, L, D_IN), dtype=jnp.float32)
        W_qkv = jax.random.normal(k2, (3 * D_IN, D_IN), dtype=jnp.float32) * D_IN ** (-0.5)
        W_o = jax.random.normal(k3, (D_IN, D_IN), dtype=jnp.float32) * D_IN ** (-0.5)
        return {'x': x, 'W_qkv': W_qkv, 'W_o': W_o}
    _L0_attn_in = _L0_attn_setup()

    def _L0_ffn_setup():
        import jax, jax.numpy as jnp
        import numpy as np
        EPS = 1e-06
        Q_B = 128.0

        def layer_norm(x):
            mean = jnp.mean(x, axis=-1, keepdims=True)
            var = jnp.var(x, axis=-1, keepdims=True)
            return (x - mean) / jnp.sqrt(var + EPS)

        def absmax_quant(x):
            gamma = jnp.max(jnp.abs(x), axis=-1, keepdims=True)
            x_hat = jnp.clip(x * Q_B / gamma, -Q_B + EPS, Q_B - EPS)
            return x_hat * gamma / Q_B

        def ternarize_weights(w):
            gamma = jnp.mean(jnp.abs(w))
            return jnp.sign(jnp.round(w / (gamma + EPS))) * gamma

        def bitlinear(x, w):
            xn = layer_norm(x)
            x_hat = xn + jax.lax.stop_gradient(absmax_quant(xn) - xn)
            w_hat = w + jax.lax.stop_gradient(ternarize_weights(w) - w)
            return jnp.einsum('bsd,od->bso', x_hat, w_hat)
        key = jax.random.key(seed)
        k1, k2, k3 = jax.random.split(key, 3)
        B, S, D = (4, 512, 512)
        x = jax.random.normal(k1, (B, S, D), dtype=jnp.float32)
        w_fc = jax.random.normal(k2, (4 * D, D), dtype=jnp.float32) / np.sqrt(D)
        w_proj = jax.random.normal(k3, (D, 4 * D), dtype=jnp.float32) / np.sqrt(4 * D)
        return {'x': x, 'w_fc': w_fc, 'w_proj': w_proj}
    _L0_ffn_in = _L0_ffn_setup()
    _d = {'L0_attn_x': _L0_attn_in['x'], 'L0_attn_W_qkv': _L0_attn_in['W_qkv'], 'L0_attn_W_o': _L0_attn_in['W_o'], 'L0_ffn_w_fc': _L0_ffn_in['w_fc'], 'L0_ffn_w_proj': _L0_ffn_in['w_proj']}
    _x0 = _d['L0_attn_x']
    _d['L0_attn_x'] = jax.random.normal(jax.random.fold_in(jax.random.key(seed), 1), (8, 1024, 512), dtype=_x0.dtype)
    del _x0
    return _d

def reference(L0_attn_x, L0_attn_W_qkv, L0_attn_W_o, L0_ffn_w_fc, L0_ffn_w_proj):

    def _L0_attn_ref(x, W_qkv, W_o):
        import jax, jax.numpy as jnp
        import numpy as np
        H = 16
        D_IN = 512
        D_H = D_IN // H
        b, L, _ = x.shape
        qkv = jnp.einsum('bld,ed->ble', x, W_qkv)
        qkv = qkv.reshape(b, 3, H, L, D_H)
        Q, K, V = (qkv[:, 0], qkv[:, 1], qkv[:, 2])
        scores = jnp.einsum('bhqd,bhkd->bhqk', Q, K) * D_H ** (-0.5)
        attn = jax.nn.softmax(scores, axis=-1)
        out = jnp.einsum('bhqk,bhkd->bhqd', attn, V)
        out = out.transpose(0, 2, 1, 3).reshape(b, L, D_IN)
        return jnp.einsum('bld,ed->ble', out, W_o)

    def _L0_ffn_ref(x, w_fc, w_proj):
        import jax, jax.numpy as jnp
        import numpy as np
        EPS = 1e-06
        Q_B = 128.0

        def layer_norm(x):
            mean = jnp.mean(x, axis=-1, keepdims=True)
            var = jnp.var(x, axis=-1, keepdims=True)
            return (x - mean) / jnp.sqrt(var + EPS)

        def absmax_quant(x):
            gamma = jnp.max(jnp.abs(x), axis=-1, keepdims=True)
            x_hat = jnp.clip(x * Q_B / gamma, -Q_B + EPS, Q_B - EPS)
            return x_hat * gamma / Q_B

        def ternarize_weights(w):
            gamma = jnp.mean(jnp.abs(w))
            return jnp.sign(jnp.round(w / (gamma + EPS))) * gamma

        def bitlinear(x, w):
            xn = layer_norm(x)
            x_hat = xn + jax.lax.stop_gradient(absmax_quant(xn) - xn)
            w_hat = w + jax.lax.stop_gradient(ternarize_weights(w) - w)
            return jnp.einsum('bsd,od->bso', x_hat, w_hat)
        h = bitlinear(x, w_fc)
        h = jax.nn.gelu(h, approximate=False)
        return bitlinear(h, w_proj)
    x = L0_attn_x
    xn = _layernorm(x, axis=-1)
    x = x + _L0_attn_ref(xn, L0_attn_W_qkv, L0_attn_W_o) + _L0_ffn_ref(xn, L0_ffn_w_fc, L0_ffn_w_proj)
    return x

_drawn_inputs = setup_inputs


def setup_inputs(seed=0):
    import zlib

    import numpy as np

    out = dict(_drawn_inputs(seed))
    spreads = {}
    factors = {}
    for name, (base, spread) in spreads.items():
        noise = np.random.default_rng([zlib.crc32(name.encode()), seed]).standard_normal(out[name].shape)
        drawn = base * np.exp(spread * noise) if base else spread * noise
        out[name] = jnp.asarray(drawn.astype(out[name].dtype))
    for name, factor in factors.items():
        out[name] = (out[name] * factor).astype(out[name].dtype)
    return out
```

```python
from contextlib import ExitStack

import concourse.bass as bass
from concourse import mybir

F32 = mybir.dt.float32
F32R = mybir.dt.float32r
F16 = mybir.dt.float16
ALU = mybir.AluOpType
ACT = mybir.ActivationFunctionType
AX = mybir.AxisListType

P = 128
B, L, D = 8, 1024, 512
H, DH = 16, 32
F = 4 * D
E3 = 3 * D
CD = D // P
CF = F // P
EPS_LN = 1e-5
EPS_BIT = 1e-6
TOP = 1024.0
BANK = 512

TT = 512
STEPS = B * L // TT
UNITS1 = CF // 2
THIRDS = E3 // BANK

HG = 4
GROUPS = B * H // HG
KT_N = L // P
UNITS = 2 * KT_N
STACK = 3 * DH
AUG = STACK + 2
HEAD = L * DH
POOLED = 6


def lin(g, k, c=0):
    if isinstance(g, int):
        return k * g + c
    r, a, o = g
    return r * (a * k) + (o * k + c)


def shift(g, d):
    return g + d if isinstance(g, int) else (g[0], g[1], g[2] + d)


def wait(eng, sem, value):
    if not isinstance(value, int) or value > 0:
        eng.wait_ge(sem, value)


def weight_stage(nc, W_qkv, W_o, w_fc, w_proj, keep):
    n_w = F * D
    with ExitStack() as ctx:
        sb = lambda name, shape, dt=F32: ctx.enter_context(nc.sbuf_tensor(name, shape, dt))
        sem = lambda name: ctx.enter_context(nc.semaphore(name))
        wqkv = sb("wqkv_rows", [P, 12, D])
        wo = sb("wo_rows", [P, 4, D])
        wfc = sb("wfc_rows", [P, CF, D])
        wproj = sb("wproj_rows", [P, CD, F])
        t1 = sb("ternary_fc_rows", [P, CF, D], F16)
        t2 = sb("ternary_proj_rows", [P, CD, F], F16)
        id32 = keep["id32"]
        id16 = sb("id16", [P, P], F16)
        ones16 = sb("ones16", [P, P], F16)
        part = sb("per_partition", [P, 4])
        total = sb("over_partitions", [P, 4])
        thr = sb("thresholds", [P, 6])
        ps = ctx.enter_context(nc.psum_tensor("weight_psum", [P, 4, BANK], F32))
        ps16 = ctx.enter_context(nc.psum_tensor("weight_psum16", [P, 3, 2 * BANK], F16))
        psw = ctx.enter_context(nc.psum_tensor("colsum_psum", [P, BANK], F32))
        ld = {k: sem(f"loaded_{k}") for k in ("qkv", "fc", "o", "proj")}
        ident, parts, reduced, step = sem("ident"), sem("parts"), sem("reduced"), sem("vector_step")
        scaled = sem("scaled")
        full32, hi_out, free32 = sem("full32"), sem("hi_out"), sem("free32")
        tern, full16, out16 = sem("ternary_ready"), sem("full16"), sem("out16")
        wo_full, wo_out = sem("wo_full"), sem("wo_out")
        cs_full, cs_out = sem("colsum_full"), sem("colsum_out")
        S = keep["scal"]
        block = ctx.enter_context(nc.Block())
        u32 = [(c, j) for c in range(CD) for j in range(THIRDS)]

        @block.sync
        def _(sp):
            sp.dma_start(wqkv[:], W_qkv.rearrange("(j p) d -> p j d", p=P)).then_inc(ld["qkv"], 16)
            sp.dma_start(wfc[:], w_fc.rearrange("(j p) d -> p j d", p=P)).then_inc(ld["fc"], 16)
            sp.dma_start(wproj[:], w_proj.rearrange("(j p) f -> p j f", p=P)).then_inc(ld["proj"], 16)
            sp.dma_start(wo[:], W_o.rearrange("(j p) d -> p j d", p=P)).then_inc(ld["o"], 16)

        @block.gpsimd
        def _(pool):
            nc.gpsimd.memset(id32[:], 0.0)
            nc.gpsimd.memset(id16[:], 0.0).then_inc(ident, 1)
            pool.wait_ge(ident, 1)
            for m in (id32, id16):
                nc.gpsimd.affine_select(out=m[:], in_=m[:], compare_op=ALU.not_equal, fill=1.0, base=0,
                                        pattern=[[-1, P]], channel_multiplier=1).then_inc(ident, 1)
            for k, value in enumerate((-0.5, EPS_LN, EPS_BIT)):
                nc.gpsimd.memset(keep["powers"][:, 4 * k:4 * k + 4], value)
            nc.gpsimd.memset(ones16[:], 1.0)
            nc.gpsimd.memset(keep["ones32"][:], 1.0).then_inc(ident, 1)
            for k, op in enumerate((bass.bass_isa.ReduceOp.max, bass.bass_isa.ReduceOp.add, bass.bass_isa.ReduceOp.add)):
                pool.wait_ge(parts, k + 1)
                nc.gpsimd.partition_all_reduce(total[:, k:k + 1], part[:, k:k + 1], P, op).then_inc(reduced, 1)

        @block.vector
        def _(dve):
            count = [0]

            def link(ins):
                count[0] += 1
                ins.then_inc(step, 1)
                dve.wait_ge(step, count[0])

            dve.wait_ge(ld["qkv"], 16)
            nc.vector.tensor_reduce(part[:, 0:1], wqkv[:], axis=AX.XY, op=ALU.max,
                                    apply_absolute_value=True).then_inc(parts, 1)
            dve.wait_ge(reduced, 1)
            link(nc.vector.tensor_scalar(S["unscale"], total[:, 0:1], 1e-30, 1.0 / TOP, ALU.max, ALU.mult))
            nc.vector.reciprocal(S["scale"], S["unscale"]).then_inc(scaled, 1)
            dve.wait_ge(scaled, 1)

            def low_parts():
                for u, (c, j) in enumerate(u32):
                    dve.wait_ge(hi_out, u + 1)
                    cols = slice(j * BANK, (j + 1) * BANK)
                    nc.vector.scalar_tensor_tensor(keep["wl"][:, c, cols], ps[:, u % 4, :], S["scale"],
                                                   keep["wh"][:, c, cols], ALU.mult, ALU.subtract).then_inc(free32, 1)

            def ternary(k, name, rows, out, thr0, gamma):
                dve.wait_ge(ld[name], 16)
                flat = rows[:].rearrange("p a b -> p (a b)")
                nc.vector.tensor_reduce(part[:, k:k + 1], rows[:], axis=AX.XY, op=ALU.add,
                                        apply_absolute_value=True).then_inc(parts, 1)
                dve.wait_ge(reduced, k + 1)
                link(nc.vector.tensor_scalar(gamma, total[:, k:k + 1], 1.0 / n_w, None, ALU.mult))
                link(nc.vector.tensor_scalar(thr[:, thr0:thr0 + 1], gamma, EPS_BIT, 0.5, ALU.add, ALU.mult))
                link(nc.vector.tensor_scalar(thr[:, thr0 + 1:thr0 + 2], thr[:, thr0:thr0 + 1], -1.0, None, ALU.mult))
                tern_rows = out[:].rearrange("p a b -> p (a b)")
                link(nc.vector.tensor_scalar(tern_rows, flat, thr[:, thr0 + 1:thr0 + 2], None, ALU.is_lt))
                nc.vector.scalar_tensor_tensor(tern_rows, flat, thr[:, thr0:thr0 + 1], tern_rows,
                                               ALU.is_gt, ALU.subtract).then_inc(tern, 1)
                dve.wait_ge(tern, k)

            ternary(1, "fc", wfc, t1, 0, S["gamma1"])
            low_parts()
            ternary(2, "proj", wproj, t2, 2, S["gamma2"])
            link(nc.vector.reciprocal(S["inv1"], S["gamma1"]))
            link(nc.vector.tensor_scalar(S["ninv1"], S["inv1"], -1.0, None, ALU.mult))
            nc.vector.tensor_tensor(S["gamma12"], S["gamma1"], S["gamma2"], ALU.mult)
            for c in range(CD):
                dve.wait_ge(wo_full, c + 1)
                nc.vector.tensor_copy(keep["woT"][:, c, :], ps[:, c, :]).then_inc(wo_out, 1)
            dve.wait_ge(cs_full, 1)
            nc.vector.tensor_copy(keep["colsum"][:], psw[:]).then_inc(cs_out, 1)

        @block.tensor
        def _(pe):
            pe.wait_ge(ident, 4)
            pe.wait_ge(ld["qkv"], 16)
            for u, (c, j) in enumerate(u32):
                wait(pe, free32, u - 3)
                for r in range(4):
                    last = nc.tensor.transpose(ps[:, u % 4, r * P:(r + 1) * P],
                                               wqkv[:, 4 * j + r, c * P:(c + 1) * P], id32[:])
                last.then_inc(full32, 1)

            def unit16(u, tiles):
                wait(pe, out16, u - 2)
                for r, tile in enumerate(tiles):
                    last = nc.tensor.transpose(ps16[:, u % 3, r * P:(r + 1) * P], tile, id16[:])
                last.then_inc(full16, 1)

            pe.wait_ge(tern, 1)
            for u in range(16):
                c, j = u % 4, u // 4
                unit16(u, [t1[:, 4 * j + r, c * P:(c + 1) * P] for r in range(4)])
            pe.wait_ge(tern, 2)
            for f in range(CF):
                unit16(16 + f, [t2[:, r, f * P:(f + 1) * P] for r in range(4)])
            pe.wait_ge(free32, len(u32))
            pe.wait_ge(ld["o"], 16)
            for c in range(CD):
                for r in range(4):
                    last = nc.tensor.transpose(ps[:, c, r * P:(r + 1) * P], wo[:, r, c * P:(c + 1) * P], id32[:])
                last.then_inc(wo_full, 1)
            pe.wait_ge(out16, 16 + CF)
            for f in range(CF):
                last = nc.tensor.matmul(psw[:], ones16[:], keep["t2T"][:, f, :], start=(f == 0), stop=(f == CF - 1))
            last.then_inc(cs_full, 1)

        @block.scalar
        def _(act):
            act.wait_ge(scaled, 1)
            for u, (c, j) in enumerate(u32):
                act.wait_ge(full32, u + 1)
                nc.scalar.activation(keep["wh"][:, c, j * BANK:(j + 1) * BANK], ps[:, u % 4, :], ACT.Copy,
                                     scale=S["scale"]).then_inc(hi_out, 1)
            for u in range(16):
                c, j = u % 4, u // 4
                act.wait_ge(full16, u + 1)
                nc.scalar.copy(keep["t1T"][:, c, j * 4 * P:(j + 1) * 4 * P], ps16[:, u % 3, 0:4 * P]).then_inc(out16, 1)
            for f in range(CF):
                act.wait_ge(full16, 16 + f + 1)
                nc.scalar.copy(keep["t2T"][:, f, :], ps16[:, (16 + f) % 3, 0:4 * P]).then_inc(out16, 1)


def token_stage(nc, x, qkv_dram, yx_dram, keep):
    x_v = x.rearrange("(t p i) d -> t p i d", p=P, i=4)
    yx_v = yx_dram.rearrange("(t p i) d -> t p i d", p=P, i=4)
    qkv_v = qkv_dram.rearrange("(t p i) e -> t p i e", p=P, i=4)
    with ExitStack() as ctx:
        sb = lambda name, shape, dt=F32: ctx.enter_context(nc.sbuf_tensor(name, shape, dt))
        sem = lambda name: ctx.enter_context(nc.semaphore(name))
        xs = sb("x_rows", [P, 2, 4, D])
        x2 = sb("x_normed", [P, 4, D])
        xh = sb("x_hi", [P, 2, CD, TT], F16)
        xl = sb("x_lo", [P, 2, CD, TT], F16)
        g = sb("gelu_out", [P, 4, 2 * BANK])
        sq = sb("gelu_squared", [P, 2, 2 * BANK])
        gacc = sb("gelu_sum", [P, 2 * BANK])
        sqacc = sb("square_sum", [P, 2 * BANK])
        hh = sb("h_hi", [P, CF, TT], F16)
        hl = sb("h_lo", [P, CF, TT], F16)
        qkv = sb("qkv_rows", [P, 2, E3])
        cen = sb("centred", [P, D])
        bn = sb("bn", [P, 4, 6])
        mv = sb("mean_var", [P, 4, 2])
        sm = sb("norm_small", [P, 8, 4])
        rc = sb("qkv_scale", [P, 2, 4])
        st = sb("hidden_stats", [P, 8, 4])
        psA = ctx.enter_context(nc.psum_tensor("psA", [P, 4, BANK], F32))
        psB = ctx.enter_context(nc.psum_tensor("psB", [P, 2, BANK], F32))
        psC = ctx.enter_context(nc.psum_tensor("psC", [P, 2, BANK], F32))
        x_loaded = [sem("x_loaded0"), sem("x_loaded1")]
        y_stored = [sem("y_stored0"), sem("y_stored1")]
        qkv_stored = [sem("qkv_stored0"), sem("qkv_stored1")]
        bn_done, mv_ready, pool_step, norm_ready = sem("bn_done"), sem("mv_ready"), sem("pool_step"), sem("norm_ready")
        x2_ready, t_full, xh_ready, xl_ready = sem("x2_ready"), sem("t_full"), sem("xh_ready"), sem("xl_ready")
        a_full, g_ready, sq_ready = sem("a_full"), sem("g_ready"), sem("sq_ready")
        hh_ready, hl_ready = sem("hh_ready"), sem("hl_ready")
        g_added, sq_added = sem("g_added"), sem("sq_added")
        b_full, b_out = sem("qkv_full"), sem("qkv_out")
        st_full, st_out, st_step, var_ready, rs_ready = sem("st_full"), sem("st_out"), sem("st_step"), sem("var_ready"), sem("rs_ready")
        y_full, cen_ready, y_ready = sem("y_full"), sem("cen_ready"), sem("y_ready")
        S = keep["scal"]
        block = ctx.enter_context(nc.Block())
        last_adds = UNITS1 - 1
        PS = 9
        VS = 6

        def steps(eng, body):
            body(0, 0, True)
            body(1, 1, True)
            with eng.Fori(1, STEPS // 2 - 1) as n:
                body((n, 2, 0), 0, True)
                body((n, 2, 1), 1, True)
            body(STEPS - 2, 0, True)
            body(STEPS - 1, 1, False)

        def turn(t, k):
            return k * (t // 2) if isinstance(t, int) else t[0] * k + (t[2] // 2) * k

        def at(t):
            return t if isinstance(t, int) else t[0] * t[1] + t[2]

        @block.sync
        def _(sp):
            sp.dma_start(xs[:, 0], x_v[0]).then_inc(x_loaded[0], 16)

            def body(t, s, has_next):
                if has_next:
                    nxt = shift(t, 1)
                    wait(sp, y_stored[1 - s], turn(nxt, 16))
                    sp.dma_start(xs[:, 1 - s], x_v[at(nxt)]).then_inc(x_loaded[1 - s], 16)
                for i in range(4):
                    sp.wait_ge(b_out, lin(t, 12, 3 * i + 3))
                    sp.dma_start(qkv_v[at(t)][:, i, :], qkv[:, i % 2, :]).then_inc(qkv_stored[i % 2], 16)
                sp.wait_ge(y_ready, lin(t, 4, 4))
                sp.dma_start(yx_v[at(t)], xs[:, s]).then_inc(y_stored[s], 16)

            steps(sp, body)
            for k in range(2):
                sp.wait_ge(y_stored[k], 16 * STEPS // 2)
                sp.wait_ge(qkv_stored[k], 16 * STEPS * 2)

        @block.gpsimd
        def _(pool):
            def norm(t, s):
                k = [0]

                def link(ins):
                    k[0] += 1
                    ins.then_inc(pool_step, 1)
                    pool.wait_ge(pool_step, lin(t, PS, k[0]))

                var = mv[:, :, 1]
                v1, r1, a, v2, v2e, r2 = (sm[:, j, :] for j in range(6))
                pool.wait_ge(mv_ready, lin(t, 1, 1))
                link(nc.gpsimd.tensor_tensor(v1, var, keep["powers"][:, 4:8], ALU.add))
                link(nc.gpsimd.tensor_tensor(r1, v1, keep["powers"][:, 0:4], ALU.pow))
                link(nc.gpsimd.tensor_tensor(a, var, r1, ALU.mult))
                link(nc.gpsimd.tensor_tensor(v2, a, r1, ALU.mult))
                link(nc.gpsimd.tensor_tensor(v2e, v2, keep["powers"][:, 8:12], ALU.add))
                link(nc.gpsimd.tensor_tensor(r2, v2e, keep["powers"][:, 0:4], ALU.pow))
                link(nc.gpsimd.tensor_tensor(sm[:, 6, :], r1, r2, ALU.mult))
                link(nc.gpsimd.tensor_tensor(a, v2e, r2, ALU.mult))
                link(nc.gpsimd.tensor_tensor(rc[:, s, :], a, S["unscale"].to_broadcast([P, 4]), ALU.mult))

            def body(t, s, has_next):
                if has_next:
                    norm(shift(t, 1), 1 - s)
                for j in range(1, UNITS1):
                    pool.wait_ge(g_ready, lin(t, UNITS1, j + 1))
                    if j == 1:
                        wait(pool, st_full, lin(t, 1))
                    else:
                        pool.wait_ge(g_added, lin(t, last_adds, j - 1))
                    nc.gpsimd.tensor_tensor(gacc[:], g[:, 0, :] if j == 1 else gacc[:], g[:, j % 4, :],
                                            ALU.add).then_inc(g_added, 1)
                pool.wait_ge(var_ready, lin(t, 1, 1))
                nc.gpsimd.tensor_tensor(st[:, 5, :], st[:, 4, :], keep["powers"][:, 0:4], ALU.pow).then_inc(rs_ready, 1)

            norm(0, 0)
            steps(pool, body)

        @block.vector
        def _(dve):
            def stats(t, s):
                dve.wait_ge(x_loaded[s], turn(t, 16) + 16)
                for i in range(4):
                    last = nc.vector.bn_stats(bn[:, i, :], xs[:, s, i, :])
                last.then_inc(bn_done, 1)
                dve.wait_ge(bn_done, lin(t, 1, 1))
                nc.vector.memset(sm[:, 7, 0:1], 0.0)
                for i in range(4):
                    last = nc.vector.bn_aggr(mv[:, i, :], bn[:, i, :])
                last.then_inc(mv_ready, 1)

            def normed(t, s):
                dve.wait_ge(pool_step, lin(t, PS, PS))
                dve.wait_ge(mv_ready, lin(t, 1, 1))
                wait(dve, t_full, lin(t, 4))
                for i in range(4):
                    last = nc.vector.tensor_scalar(x2[:, i, :], xs[:, s, i, :], mv[:, i, 0:1], sm[:, 6, i:i + 1],
                                                   ALU.subtract, ALU.mult)
                last.then_inc(x2_ready, 1)

            def low(t, s):
                for c in range(CD):
                    dve.wait_ge(xh_ready, lin(t, 4, c + 1))
                    nc.vector.tensor_tensor(xl[:, s, c, :], psC[:, (1 - s + c) % 2, :], xh[:, s, c, :],
                                            ALU.subtract).then_inc(xl_ready, 1)

            def add_square(t, j):
                dve.wait_ge(sq_ready, lin(t, UNITS1, j + 1))
                if j == 1:
                    wait(dve, st_full, lin(t, 1))
                else:
                    dve.wait_ge(sq_added, lin(t, last_adds, j - 1))
                nc.vector.tensor_tensor(sqacc[:], sq[:, 0, :] if j == 1 else sqacc[:], sq[:, j % 2, :],
                                        ALU.add).then_inc(sq_added, 1)

            def body(t, s, has_next):
                if has_next:
                    stats(shift(t, 1), 1 - s)
                wait(dve, y_full, lin(t, 4))
                for j in range(UNITS1):
                    dve.wait_ge(g_ready, lin(t, UNITS1, j + 1))
                    pair = slice(2 * j, 2 * j + 2)
                    gj = g[:, j % 4, :].rearrange("p (a b) -> p a b", a=2)
                    nc.vector.tensor_scalar(hh[:, pair, :], gj, S["inv1"], None, ALU.mult).then_inc(hh_ready, 1)
                    if j >= 2:
                        add_square(t, j - 1)
                    dve.wait_ge(hh_ready, lin(t, UNITS1, j + 1))
                    nc.vector.scalar_tensor_tensor(hl[:, pair, :], gj, S["inv1"], hh[:, pair, :],
                                                   ALU.mult, ALU.subtract).then_inc(hl_ready, 1)
                    if j == 4 and has_next:
                        normed(shift(t, 1), 1 - s)
                add_square(t, UNITS1 - 1)
                if has_next:
                    low(shift(t, 1), 1 - s)

                k = [0]

                def link(ins):
                    k[0] += 1
                    ins.then_inc(st_step, 1)
                    dve.wait_ge(st_step, lin(t, VS, k[0]))

                dve.wait_ge(st_full, lin(t, 1, 1))
                nc.vector.tensor_scalar(st[:, 0:2, :], psC[:, (s + 4) % 2, 0:8].rearrange("p (a b) -> p a b", a=2),
                                        1.0 / F, None, ALU.mult).then_inc(st_out, 1)
                dve.wait_ge(st_out, lin(t, 1, 1))
                mean, ms, var, var_eps, rs, rv, ratio = (st[:, j, :] for j in (0, 1, 2, 4, 5, 3, 6))
                link(nc.vector.tensor_tensor(var, mean, mean, ALU.mult))
                link(nc.vector.tensor_tensor(var, ms, var, ALU.subtract))
                link(nc.vector.tensor_scalar(var, var, 0.0, None, ALU.max))
                nc.vector.tensor_scalar(var_eps, var, EPS_BIT, None, ALU.add).then_inc(var_ready, 1)
                link(nc.vector.reciprocal(rv, var))
                nc.vector.tensor_scalar(mean, mean, S["ninv1"], None, ALU.mult)
                link(nc.vector.tensor_tensor(ratio, var, rv, ALU.mult))
                dve.wait_ge(rs_ready, lin(t, 1, 1))
                link(nc.vector.scalar_tensor_tensor(st[:, 7, :], rs, S["gamma12"], ratio, ALU.mult, ALU.mult))
                for i in range(4):
                    dve.wait_ge(y_full, lin(t, 4, i + 1))
                    if i:
                        dve.wait_ge(y_ready, lin(t, 4, i))
                    else:
                        wait(dve, y_ready, lin(t, 4))
                    nc.vector.scalar_tensor_tensor(cen[:], keep["colsum"][:], st[:, 0, i:i + 1],
                                                   psC[:, (s + 5 + i) % 2, :], ALU.mult, ALU.add).then_inc(cen_ready, 1)
                    dve.wait_ge(cen_ready, lin(t, 4, i + 1))
                    nc.vector.scalar_tensor_tensor(xs[:, s, i, :], cen[:], st[:, 7, i:i + 1], xs[:, s, i, :],
                                                   ALU.mult, ALU.add).then_inc(y_ready, 1)

            stats(0, 0)
            normed(0, 0)
            low(0, 0)
            steps(dve, body)

        @block.scalar
        def _(act):
            def high(t, s):
                for c in range(CD):
                    act.wait_ge(t_full, lin(t, 4, c + 1))
                    nc.scalar.copy(xh[:, s, c, :], psC[:, (1 - s + c) % 2, :]).then_inc(xh_ready, 1)

            def square(t, j):
                act.wait_ge(g_ready, lin(t, UNITS1, j + 1))
                if j >= 2:
                    act.wait_ge(sq_added, lin(t, last_adds, max(j - 2, 1)))
                else:
                    wait(act, sq_added, lin(t, last_adds))
                nc.scalar.activation(sq[:, j % 2, :], g[:, j % 4, :], ACT.Square).then_inc(sq_ready, 1)

            def body(t, s, has_next):
                for j in range(UNITS1):
                    act.wait_ge(a_full, lin(t, UNITS1, j + 1))
                    if j >= 4:
                        act.wait_ge(hl_ready, lin(t, UNITS1, j - 3))
                        act.wait_ge(g_added, lin(t, last_adds, max(j - 4, 1)))
                    else:
                        wait(act, hl_ready, lin(t, UNITS1, j - 3))
                        wait(act, g_added, lin(t, last_adds, j - 3))
                    nc.scalar.activation(g[:, j % 4, :], psA[:, 2 * (j % 2):2 * (j % 2) + 2, :], ACT.Gelu,
                                         scale=S["gamma1"]).then_inc(g_ready, 1)
                    if j:
                        square(t, j - 1)
                square(t, UNITS1 - 1)
                for u in range(12):
                    i, third = divmod(u, THIRDS)
                    if u == 6 and has_next:
                        high(shift(t, 1), 1 - s)
                    act.wait_ge(b_full, lin(t, 12, u + 1))
                    if third == 0:
                        wait(act, qkv_stored[i % 2], lin(t, 32, 16 * (i // 2)))
                    act.wait_ge(pool_step, lin(t, PS, PS))
                    nc.scalar.activation(qkv[:, i % 2, third * BANK:(third + 1) * BANK], psB[:, u % 2, :], ACT.Copy,
                                         scale=rc[:, s, i:i + 1]).then_inc(b_out, 1)

            high(0, 0)
            steps(act, body)

        @block.tensor
        def _(pe):
            def transposes(t, s, first=False):
                pe.wait_ge(x2_ready, lin(t, 1, 1))
                for c in range(CD):
                    if c >= 2:
                        pe.wait_ge(xl_ready, lin(t, 4, c - 1))
                    elif not first:
                        wait(pe, cen_ready, lin(t, 4, c - 5))
                    for i in range(4):
                        last = nc.tensor.transpose(psC[:, (1 - s + c) % 2, i * P:(i + 1) * P],
                                                   x2[:, i, c * P:(c + 1) * P], keep["id32"][:])
                    last.then_inc(t_full, 1)

            def body(t, s, has_next):
                pe.wait_ge(xl_ready, lin(t, 4, 4))
                for j in range(UNITS1):
                    wait(pe, g_ready, lin(t, UNITS1, j - 1))
                    for b in range(2):
                        f = 2 * j + b
                        for c in range(CD):
                            w = keep["t1T"][:, c, f * P:(f + 1) * P]
                            for k, xx in enumerate((xh, xl)):
                                last = nc.tensor.matmul(psA[:, 2 * (j % 2) + b, :], w, xx[:, s, c, :],
                                                        start=(c == 0 and k == 0), stop=(c == CD - 1 and k == 1))
                    last.then_inc(a_full, 1)
                for u in range(12):
                    i, third = divmod(u, THIRDS)
                    if u == 6 and has_next:
                        transposes(shift(t, 1), 1 - s)
                    wait(pe, b_out, lin(t, 12, u - 1))
                    cols = slice(third * BANK, (third + 1) * BANK)
                    terms = [(xx, ww, c) for c in range(CD) for xx, ww in ((xh, "wh"), (xh, "wl"), (xl, "wh"))]
                    for k, (xx, ww, c) in enumerate(terms):
                        last = nc.tensor.matmul(psB[:, u % 2, :], xx[:, s, c, i * P:(i + 1) * P], keep[ww][:, c, cols],
                                                start=(k == 0), stop=(k == len(terms) - 1))
                    last.then_inc(b_full, 1)
                pe.wait_ge(g_added, lin(t, last_adds, last_adds))
                pe.wait_ge(sq_added, lin(t, last_adds, last_adds))
                if has_next:
                    pe.wait_ge(xl_ready, lin(t, 4, 8))
                else:
                    pe.wait_ge(cen_ready, lin(t, 4))
                for q, acc in enumerate((gacc, sqacc)):
                    for i in range(4):
                        for b in range(2):
                            last = nc.tensor.matmul(psC[:, (s + 4) % 2, 4 * q + i:4 * q + i + 1],
                                                    acc[:, b * BANK + i * P:b * BANK + (i + 1) * P],
                                                    keep["ones32"][:, 0:1], start=(b == 0), stop=(b == 1))
                last.then_inc(st_full, 1)
                pe.wait_ge(hl_ready, lin(t, UNITS1, UNITS1))
                for i in range(4):
                    if i == 1:
                        pe.wait_ge(st_out, lin(t, 1, 1))
                    elif i >= 2:
                        pe.wait_ge(cen_ready, lin(t, 4, i - 1))
                    for f in range(CF):
                        for k, h in enumerate((hh, hl)):
                            last = nc.tensor.matmul(psC[:, (s + 5 + i) % 2, :], h[:, f, i * P:(i + 1) * P],
                                                    keep["t2T"][:, f, :], start=(f == 0 and k == 0),
                                                    stop=(f == CF - 1 and k == 1))
                    last.then_inc(y_full, 1)

            transposes(0, 0, first=True)
            steps(pe, body)


MISC = {1: [("T", 0, 0), ("T", 0, 1), ("T", 0, 2)], 2: [("T", 0, 3), ("D", 1, 1)],
        3: [("T", 1, 0), ("T", 1, 1)], 4: [("T", 1, 2), ("T", 1, 3)],
        5: [("T", 2, 0), ("T", 2, 1)], 6: [("T", 2, 2), ("T", 2, 3)],
        7: [("A", 0), ("T", 3, 0)], 8: [("T", 3, 1), ("T", 3, 2)], 9: [("T", 3, 3)],
        10: [("A", 1), ("D", 0, 0)], 12: [("A", 2)], 15: [("A", 3)]}
MAXIMA = [0, 0, 0] + [6] * 9 + [5] * 2 + [0] * 2
BUILD = {0: [0, 1], 3: [2], 5: [3]}


def attention_stage(nc, qkv_dram, ot_dram, keep):
    per_head = 2 * KT_N
    scale = DH ** -0.5
    blocks = qkv_dram.rearrange("t e -> (t e)").rearrange("(m h p x) -> m p h x", h=HG, p=P, x=HEAD // P)
    with ExitStack() as ctx:
        sb = lambda name, shape, dt=F32: ctx.enter_context(nc.sbuf_tensor(name, shape, dt))
        sem = lambda name: ctx.enter_context(nc.semaphore(name))
        qn = sb("q_rows", [P, HG, KT_N, DH])
        kn = sb("k_rows", [P, HG, KT_N, DH])
        v = sb("v_rows", [P, 2, HG, KT_N, DH])
        qs = sb("q_stack", [P, 2, KT_N, 3, DH])
        ks = sb("k_stack", [P, 2, KT_N, 3, DH])
        qT = sb("q_stackT", [P, 2, HG, L], F32R)
        kT = sb("k_stackT", [P, 2, HG, L], F32R)
        pr = sb("probs", [P, 8, HG, BANK])
        acc = sb("probs_sum", [P, 2, HG, BANK])
        oraw = sb("out_raw", [P, 2, BANK])
        rden = sb("inverse_denominators", [P, BANK])
        on = sb("out_normed", [P, 2, BANK])
        mx = sb("half_maxima", [P, HG, KT_N, 2])
        nm = sb("negated_maxima", [P, 2, KT_N])
        au = sb("maxima_parts", [P, 2, 2, KT_N])
        rows = sb("maxima_rows", [2 * KT_N, 2, P])
        psX = ctx.enter_context(nc.psum_tensor("scores_for_maxima", [P, 2, BANK], F32))
        psS = ctx.enter_context(nc.psum_tensor("scores", [P, 2, 2, BANK], F32))
        psO = ctx.enter_context(nc.psum_tensor("outputs", [P, BANK], F32))
        psM = ctx.enter_context(nc.psum_tensor("misc", [P, BANK], F32))
        qk_loaded, v_loaded = sem("qk_loaded"), [sem("v_loaded0"), sem("v_loaded1")]
        ones_set = sem("ones_set")
        hi_ready, lo_ready = sem("hi_ready"), sem("lo_ready")
        t_full, t_out = sem("stacks_transposed"), sem("stacksT_ready")
        x_full, max_done, aug_step = sem("max_scores_full"), sem("max_done"), sem("maxima_step")
        a_full, rows_ready = sem("maxima_transposed"), sem("maxima_rows_ready")
        aug_loaded = [sem(f"maxima_loaded{h}") for h in range(HG)]
        s_full, exp_done, pv_done = sem("scores_full"), sem("exp_done"), sem("pv_done")
        added = sem("probs_added")
        d_full, d_out, oraw_out, on_ready = sem("den_full"), sem("den_out"), sem("out_raw_ready"), sem("out_normed_ready")
        ot_stored = [sem("ot_stored0"), sem("ot_stored1")]
        block = ctx.enter_context(nc.Block())

        def slot(g):
            return g % 2 if isinstance(g, int) else g[2] % 2

        def turn(g, k):
            return k * (g // 2) if isinstance(g, int) else g[0] * k + (g[2] // 2) * k

        def at(g):
            return g if isinstance(g, int) else g[0] * g[1] + g[2]

        def groups(eng, body):
            body(-1, False, True)
            body(0, True, True)
            with eng.Fori(0, (GROUPS - 4) // 2) as m:
                body((m, 2, 1), True, True)
                body((m, 2, 2), True, True)
            body(GROUPS - 3, True, True)
            body(GROUPS - 2, True, True)
            body(GROUPS - 1, True, False)

        def misc(g, w, cur, nxt):
            first = isinstance(g, int) and g <= 0
            return [e for e in MISC.get(w, [])
                    if (e[0] != "D" and nxt) or (e[0] == "D" and cur and not (e[1] and first))]

        def freed(g, e):
            if e[0] == "T":
                return t_out, lin(shift(g, 1), 4 * HG, 4 * e[1] + e[2] + 1)
            if e[0] == "A":
                return rows_ready, lin(shift(g, 1), HG, e[1] + 1)
            return d_out, lin(shift(g, -e[1]), 2, e[2] + 1)

        @block.sync
        def _(sp):
            def load_block(dst, g, section):
                group = at(g)
                return sp.dma_start(dst.rearrange("p h i d -> p h (i d)"), blocks[group + (group // 4) * 8 + 4 * section])

            def load_qk(g):
                wait(sp, lo_ready, lin(g, 2 * HG))
                load_block(qn[:], g, 0).then_inc(qk_loaded, 16)
                load_block(kn[:], g, 1).then_inc(qk_loaded, 16)

            def load_maxima(g, h):
                sp.wait_ge(rows_ready, lin(g, HG, h + 1))
                sp.dma_start(qT[STACK:AUG, slot(g), h, :].bitcast(F32).rearrange("a (i c) -> a i c", c=P),
                             rows[:, h % 2, :]).then_inc(aug_loaded[h], 16)

            def store_ot(g, hf):
                sp.wait_ge(on_ready, lin(g, 2, hf + 1))
                sp.dma_start(ot_dram[at(g)][hf], on[:, hf, :]).then_inc(ot_stored[hf], 16)

            def body(g, cur, nxt):
                n = shift(g, 1)
                if nxt:
                    wait(sp, pv_done, lin(g, UNITS))
                    load_block(v[:, slot(n)], n, 2).then_inc(v_loaded[slot(n)], 16)
                for w in range(UNITS):
                    for e in misc(g, w, cur, nxt):
                        if e[0] == "A":
                            load_maxima(n, e[1])
                        elif e[0] == "D":
                            store_ot(shift(g, -e[1]), e[2])
                    if w == 6 and nxt and not (isinstance(g, int) and g == GROUPS - 2):
                        load_qk(shift(g, 2))

            load_qk(0)
            groups(sp, body)
            store_ot(GROUPS - 1, 1)
            for hf in range(2):
                sp.wait_ge(ot_stored[hf], 16 * GROUPS)

        @block.gpsimd
        def _(pool):
            nc.gpsimd.memset(qT[96:P, :, :, :].bitcast(F32), 0.0)
            nc.gpsimd.memset(kT[96:P, :, :, :].bitcast(F32), 1.0).then_inc(ones_set, 1)

            def body(g, cur, nxt):
                if not cur:
                    return
                for hf in range(2):
                    wait(pool, d_full, lin(g, 2, hf - 1))
                    for j in range(1, POOLED):
                        pool.wait_ge(exp_done, lin(g, 2 * UNITS, 2 * (8 * hf + j) + 2))
                        if j > 1:
                            pool.wait_ge(added, lin(g, 2 * (POOLED - 1), (POOLED - 1) * hf + j - 1))
                        nc.gpsimd.tensor_tensor(acc[:, hf], pr[:, 0] if j == 1 else acc[:, hf], pr[:, j],
                                                ALU.add).then_inc(added, 1)

            groups(pool, body)

        @block.scalar
        def _(act):
            def build(g, h):
                act.wait_ge(qk_loaded, lin(g, 32, 32))
                wait(act, t_full, lin(g, 4 * HG, 4 * h - 4))
                for src, dst, step in ((kn, ks, 2), (qn, qs, 1)):
                    hi = dst[:, h % 2].bitcast(F32R)[:, :, 0:step + 1:step, :]
                    nc.scalar.copy(hi, src[:, h].unsqueeze(2).to_broadcast([P, KT_N, 2, DH])).then_inc(hi_ready, 1)

            def exp(g, w, hp):
                act.wait_ge(s_full, lin(g, 2 * UNITS, 2 * w + hp + 1))
                if hp == 0:
                    j, q = w % 8, w // 8 - 1
                    wait(act, pv_done, lin(g, UNITS, w - 7))
                    if j < POOLED:
                        wait(act, added, lin(g, 2 * (POOLED - 1), (POOLED - 1) * q + max(j, 1)))
                    else:
                        wait(act, d_full, lin(g, 2, q + 1))
                nc.scalar.activation(pr[:, w % 8, 2 * hp:2 * hp + 2, :], psS[:, hp], ACT.Exp,
                                     scale=scale).then_inc(exp_done, 1)

            def evacuate(g, h, q):
                act.wait_ge(t_full, lin(g, 4 * HG, 4 * h + q + 1))
                dst = (kT, qT)[q // 2]
                nc.scalar.copy(dst[0:STACK, slot(g), h, (q % 2) * BANK:(q % 2 + 1) * BANK],
                               psM[0:STACK, :]).then_inc(t_out, 1)

            def out_raw(g, hf):
                act.wait_ge(pv_done, lin(g, UNITS, 8 * hf + 8))
                wait(act, on_ready, lin(g, 2, hf - 1))
                nc.scalar.copy(oraw[:, hf, :], psO[:]).then_inc(oraw_out, 1)

            def body(g, cur, nxt):
                n = shift(g, 1)
                for w in range(UNITS):
                    stacks = [e for e in misc(g, w, cur, nxt) if e[0] == "T"]
                    if nxt and w == 0:
                        build(n, 0)
                    if cur:
                        exp(g, w, 0)
                    for e in stacks[:1]:
                        evacuate(n, e[1], e[2])
                    if cur:
                        exp(g, w, 1)
                    for e in stacks[1:]:
                        evacuate(n, e[1], e[2])
                    for h in BUILD.get(w, []) if nxt else []:
                        if h:
                            build(n, h)
                    if cur and w == 0 and not (isinstance(g, int) and g == 0):
                        out_raw(shift(g, -1), 1)
                    if cur and w == 8:
                        out_raw(g, 0)

            groups(act, body)
            out_raw(GROUPS - 1, 1)

        @block.vector
        def _(dve):
            def build(g, h):
                for k, (src, dst, hi, lo) in enumerate(((kn, ks, 0, 1), (qn, qs, 0, 2))):
                    dve.wait_ge(hi_ready, lin(g, 2 * HG, 2 * h + k + 1))
                    nc.vector.tensor_tensor(dst[:, h % 2].bitcast(F32R)[:, :, lo, :], src[:, h], dst[:, h % 2, :, hi, :],
                                            ALU.subtract).then_inc(lo_ready, 1)

            def maximum(g, r):
                dve.wait_ge(x_full, lin(g, per_head * HG, r + 1))
                h, t, kh = r // per_head, r % per_head // 2, r % 2
                nc.vector.tensor_reduce(mx[:, h, t, kh:kh + 1], psX[:, r % 2, :], axis=AX.X, op=ALU.max).then_inc(max_done, 1)

            def split_maxima(g, h):
                dve.wait_ge(max_done, lin(g, per_head * HG, per_head * (h + 1)))
                wait(dve, a_full, lin(g, HG, h - 1))
                nc.vector.tensor_reduce(nm[:, h % 2, :], mx[:, h], axis=AX.X, op=ALU.max, negate=True).then_inc(aug_step, 1)
                dve.wait_ge(aug_step, lin(g, 3 * HG, 3 * h + 1))
                nc.vector.tensor_copy(au[:, h % 2, 0, :].bitcast(F32R), nm[:, h % 2, :]).then_inc(aug_step, 1)
                dve.wait_ge(aug_step, lin(g, 3 * HG, 3 * h + 2))
                nc.vector.tensor_tensor(au[:, h % 2, 1, :].bitcast(F32R), nm[:, h % 2, :], au[:, h % 2, 0, :],
                                        ALU.subtract).then_inc(aug_step, 1)

            def copy_rows(g, h):
                dve.wait_ge(a_full, lin(g, HG, h + 1))
                wait(dve, aug_loaded[h % 2 + 2 * (1 - h // 2)], lin(g, 16, 16 * (h // 2)))
                nc.vector.tensor_copy(rows[:, h % 2, :], psM[0:2 * KT_N, 0:P]).then_inc(rows_ready, 1)

            def normalise(g, hf):
                dve.wait_ge(d_full, lin(g, 2, hf + 1))
                wait(dve, on_ready, lin(g, 2, hf))
                nc.vector.reciprocal(rden[:], psM[:]).then_inc(d_out, 1)
                dve.wait_ge(d_out, lin(g, 2, hf + 1))
                dve.wait_ge(oraw_out, lin(g, 2, hf + 1))
                wait(dve, ot_stored[hf], lin(g, 16))
                nc.vector.tensor_tensor(on[:, hf, :], oraw[:, hf, :], rden[:], ALU.mult).then_inc(on_ready, 1)

            def body(g, cur, nxt):
                n = shift(g, 1)
                r = 0
                for w in range(UNITS):
                    todo = MAXIMA[w] if nxt else 0
                    entries = [e for e in misc(g, w, cur, nxt) if e[0] != "T"]
                    for k in range(todo):
                        maximum(n, r)
                        r += 1
                        if r % per_head == 0:
                            split_maxima(n, r // per_head - 1)
                        if k == 2:
                            for e in entries[:1]:
                                finish(g, e)
                    for e in entries[1 if todo > 2 else 0:]:
                        finish(g, e)
                    for h in BUILD.get(w, []) if nxt else []:
                        build(n, h)

            def finish(g, e):
                if e[0] == "A":
                    copy_rows(shift(g, 1), e[1])
                else:
                    normalise(shift(g, -e[1]), e[2])

            groups(dve, body)
            normalise(GROUPS - 1, 1)

        @block.tensor
        def _(pe):
            def scores(g, w, hp):
                hf, i = divmod(w, KT_N)
                wait(pe, exp_done, lin(g, 2 * UNITS, 2 * w + hp - 1))
                if w == 0:
                    if hp == 0:
                        pe.wait_ge(t_out, lin(g, 4 * HG, 4 * HG))
                    for h in (2 * hp, 2 * hp + 1):
                        pe.wait_ge(aug_loaded[h], lin(g, 16, 16))
                for k in range(2):
                    h = 2 * hp + k
                    last = nc.tensor.matmul(psS[:, hp, k, :], kT[0:AUG, slot(g), h, i * P:(i + 1) * P],
                                            qT[0:AUG, slot(g), h, hf * BANK:(hf + 1) * BANK], start=True, stop=True)
                last.then_inc(s_full, 1)

            def outputs(g, w):
                hf, i = divmod(w, KT_N)
                pe.wait_ge(exp_done, lin(g, 2 * UNITS, 2 * w + 2))
                if w == 0:
                    pe.wait_ge(v_loaded[slot(g)], turn(g, 16) + 16)
                if i == 0:
                    wait(pe, oraw_out, lin(g, 2, hf))
                for h in range(HG):
                    last = nc.tensor.matmul(psO[32 * h:32 * h + 32, :], v[:, slot(g), h, i, :], pr[:, w % 8, h, :],
                                            start=(i == 0), stop=(i == KT_N - 1))
                last.then_inc(pv_done, 1)

            def max_scores(g, r):
                h, t, kh = r // per_head, r % per_head // 2, r % 2
                if r % per_head == 0:
                    pe.wait_ge(t_out, lin(g, 4 * HG, 4 * h + 4))
                wait(pe, max_done, lin(g, per_head * HG, r - 1))
                nc.tensor.matmul(psX[:, r % 2, :], qT[0:STACK, slot(g), h, t * P:(t + 1) * P],
                                 kT[0:STACK, slot(g), h, kh * BANK:(kh + 1) * BANK], start=True, stop=True).then_inc(x_full, 1)

            def entry(g, e, before):
                n = shift(g, 1)
                if before:
                    wait(pe, *before)
                if e[0] == "T":
                    _, h, q = e
                    pe.wait_ge(lo_ready, lin(n, 2 * HG, 2 * h + q // 2 + 1))
                    src = (ks, qs)[q // 2][:, h % 2].rearrange("p i r d -> p i (r d)")
                    for k in range(4):
                        last = nc.tensor.transpose(psM[0:STACK, k * P:(k + 1) * P], src[:, 4 * (q % 2) + k, :], keep["id32"][:])
                    last.then_inc(t_full, 1)
                elif e[0] == "A":
                    h = e[1]
                    pe.wait_ge(aug_step, lin(n, 3 * HG, 3 * h + 3))
                    nc.tensor.transpose(psM[0:2 * KT_N, 0:P], au[:, h % 2].rearrange("p a i -> p (a i)"),
                                        keep["id32"][:]).then_inc(a_full, 1)
                else:
                    denominators(shift(g, -e[1]), e[2])
                return freed(g, e)

            def denominators(g, hf):
                pe.wait_ge(exp_done, lin(g, 2 * UNITS, UNITS * (hf + 1)))
                pe.wait_ge(added, lin(g, 2 * (POOLED - 1), (POOLED - 1) * (hf + 1)))
                parts = [acc[:, hf]] + [pr[:, j] for j in range(POOLED, KT_N)]
                for k, part in enumerate(parts):
                    for h in range(HG):
                        last = nc.tensor.matmul(psM[32 * h:32 * h + 32, :], keep["ones32"][:, 0:32], part[:, h, :],
                                                start=(k == 0), stop=(k == len(parts) - 1))
                last.then_inc(d_full, 1)

            def body(g, cur, nxt):
                n = shift(g, 1)
                before = None
                if not (isinstance(g, int) and g < 0):
                    before = freed(shift(g, -1), ("A", 3))
                r = 0
                for w in range(UNITS):
                    entries = misc(g, w, cur, nxt)
                    if cur:
                        scores(g, w, 0)
                        scores(g, w, 1)
                    for e in entries[:1]:
                        before = entry(g, e, before)
                    todo = MAXIMA[w] if nxt else 0
                    for k in range(todo):
                        max_scores(n, r)
                        r += 1
                        if k == 2:
                            for e in entries[1:2]:
                                before = entry(g, e, before)
                            if cur:
                                finish_unit(g, w)
                    if todo <= 2:
                        for e in entries[1:2]:
                            before = entry(g, e, before)
                        if cur:
                            finish_unit(g, w)
                    for e in entries[2:]:
                        before = entry(g, e, before)

            def finish_unit(g, w):
                if w:
                    outputs(g, w - 1)
                elif not (isinstance(g, int) and g == 0):
                    outputs(shift(g, -1), UNITS - 1)

            pe.wait_ge(ones_set, 1)
            groups(pe, body)
            outputs(GROUPS - 1, UNITS - 1)
            wait(pe, *freed(GROUPS - 1, ("D", 0, 0)))
            denominators(GROUPS - 1, 1)


def output_stage(nc, ot_dram, yx_dram, out, keep):
    ot_v = ot_dram.rearrange("(b g) f p q -> b f p g q", g=HG)
    yx_v = yx_dram.rearrange("(b p f i) d -> b f p i d", p=P, f=2, i=4)
    out_v = out.rearrange("b (p f i) d -> b f p i d", p=P, f=2, i=4)
    with ExitStack() as ctx:
        sb = lambda name, shape, dt=F32: ctx.enter_context(nc.sbuf_tensor(name, shape, dt))
        sem = lambda name: ctx.enter_context(nc.semaphore(name))
        ot = sb("attention_out", [P, 2, HG, BANK])
        y = sb("x_plus_ffn", [P, 2, 4, D])
        ps = ctx.enter_context(nc.psum_tensor("projected", [P, 4, BANK], F32))
        loaded = [sem("ot_loaded0"), sem("ot_loaded1")]
        y_loaded = [sem("y_loaded0"), sem("y_loaded1")]
        stored = [sem("out_stored0"), sem("out_stored1")]
        full, summed = sem("projection_full"), sem("summed")
        block = ctx.enter_context(nc.Block())

        @block.sync
        def _(sp):
            def load(b, f, k):
                sp.dma_start(ot[:, f], ot_v[b][f]).then_inc(loaded[f], 16)
                sp.dma_start(y[:, f], yx_v[b][f]).then_inc(y_loaded[f], 16)

            load(0, 0, 0)
            load(0, 1, 0)
            with sp.Fori(1, B) as b:
                for f in range(2):
                    sp.wait_ge(summed, b * 8 + (4 * f - 4))
                    sp.dma_start(out_v[b - 1][f], y[:, f]).then_inc(stored[f], 16)
                    sp.dma_start(ot[:, f], ot_v[b][f]).then_inc(loaded[f], 16)
                    sp.wait_ge(stored[f], b * 16)
                    sp.dma_start(y[:, f], yx_v[b][f]).then_inc(y_loaded[f], 16)
            for f in range(2):
                sp.wait_ge(summed, 8 * B - 4 + 4 * f)
                sp.dma_start(out_v[B - 1][f], y[:, f]).then_inc(stored[f], 16)
            for f in range(2):
                sp.wait_ge(stored[f], 16 * B)

        @block.tensor
        def _(pe):
            def body(b):
                for f in range(2):
                    pe.wait_ge(loaded[f], lin(b, 16, 16))
                    for i in range(4):
                        wait(pe, summed, lin(b, 8, 4 * f + i - 3))
                        for c in range(CD):
                            last = nc.tensor.matmul(ps[:, i, :], ot[:, f, c, i * P:(i + 1) * P], keep["woT"][:, c, :],
                                                    start=(c == 0), stop=(c == CD - 1))
                        last.then_inc(full, 1)

            body(0)
            with pe.Fori(1, B) as b:
                body((b, 1, 0))

        @block.vector
        def _(dve):
            with dve.Fori(0, B) as b:
                for f in range(2):
                    dve.wait_ge(y_loaded[f], b * 16 + 16)
                    for i in range(4):
                        dve.wait_ge(full, b * 8 + (4 * f + i + 1))
                        nc.vector.tensor_tensor(y[:, f, i, :], ps[:, i, :], y[:, f, i, :], ALU.add).then_inc(summed, 1)


def build(nc, x, W_qkv, W_o, w_fc, w_proj, out):
    qkv_dram = nc.dram_tensor("qkv_scratch", (B * L, E3), F32).ap()
    yx_dram = nc.dram_tensor("x_plus_ffn_scratch", (B * L, D), F32).ap()
    ot_dram = nc.dram_tensor("attention_scratch", (GROUPS, 2, P, BANK), F32).ap()
    with ExitStack() as ctx:
        sb = lambda name, shape, dt=F32: ctx.enter_context(nc.sbuf_tensor(name, shape, dt))
        keep = {
            "id32": sb("id32", [P, P]), "ones32": sb("ones32", [P, 32]), "powers": sb("powers_and_epsilons", [P, 12]),
            "woT": sb("woT", [P, CD, D]),
        }
        scalars = sb("scalars", [P, 8])
        names = ("scale", "unscale", "gamma1", "gamma2", "inv1", "ninv1", "gamma12")
        keep["scal"] = {k: scalars[:, j:j + 1] for j, k in enumerate(names)}
        with ExitStack() as weights:
            wsb = lambda name, shape, dt: weights.enter_context(nc.sbuf_tensor(name, shape, dt))
            keep["wh"] = wsb("wqkvT_hi", [P, CD, E3], F16)
            keep["wl"] = wsb("wqkvT_lo", [P, CD, E3], F16)
            keep["t1T"] = wsb("ternary_fcT", [P, CD, F], F16)
            keep["t2T"] = wsb("ternary_projT", [P, CF, D], F16)
            keep["colsum"] = wsb("ternary_proj_sums", [P, D], F32)
            weight_stage(nc, W_qkv, W_o, w_fc, w_proj, keep)
            token_stage(nc, x.rearrange("b l d -> (b l) d"), qkv_dram, yx_dram, keep)
        attention_stage(nc, qkv_dram, ot_dram, keep)
        output_stage(nc, ot_dram, yx_dram, out, keep)


_INS = ["L0_attn_x", "L0_attn_W_qkv", "L0_attn_W_o", "L0_ffn_w_fc", "L0_ffn_w_proj"]


def kernel(**inputs):
    import numpy as np
    import concourse.bacc as bacc
    from concourse.bass_utils import run_bass_kernel_spmd

    nc = bacc.Bacc("TRN2", target_bir_lowering=False, num_devices=1)
    arrays, args = {}, []
    for name in _INS:
        a = np.ascontiguousarray(inputs[name])
        arrays[f"in_{name}"] = a
        args.append(nc.dram_tensor(f"in_{name}", a.shape, mybir.dt.from_np(a.dtype), kind="ExternalInput").ap())
    out = nc.dram_tensor("out_0", (B, L, D), F32, kind="ExternalOutput").ap()
    build(nc, *args, out)
    r = run_bass_kernel_spmd(nc, [arrays], core_ids=[0])
    return r.results[0]["out_0"]
```

```python
from contextlib import ExitStack

import concourse.bass as bass
from concourse import mybir

F32 = mybir.dt.float32
F32R = mybir.dt.float32r
F16 = mybir.dt.float16
ALU = mybir.AluOpType
ACT = mybir.ActivationFunctionType
AX = mybir.AxisListType

P = 128
B, L, D = 8, 1024, 512
H, DH = 16, 32
F = 4 * D
E3 = 3 * D
CD = D // P
CF = F // P
EPS_LN = 1e-5
EPS_BIT = 1e-6
TOP = 1024.0
BANK = 512

TT = 512
STEPS = B * L // TT
UNITS1 = CF // 2
THIRDS = E3 // BANK

HG = 4
GROUPS = B * H // HG
KT_N = L // P
UNITS = 2 * KT_N
STACK = 3 * DH
AUG = STACK + 2
HEAD = L * DH
POOLED = 6


def lin(g, k, c=0):
    if isinstance(g, int):
        return k * g + c
    r, a, o = g
    return r * (a * k) + (o * k + c)


def shift(g, d):
    return g + d if isinstance(g, int) else (g[0], g[1], g[2] + d)


def wait(eng, sem, value):
    if not isinstance(value, int) or value > 0:
        eng.wait_ge(sem, value)


def weight_stage(nc, W_qkv, W_o, w_fc, w_proj, keep):
    n_w = F * D
    with ExitStack() as ctx:
        sb = lambda name, shape, dt=F32: ctx.enter_context(nc.sbuf_tensor(name, shape, dt))
        sem = lambda name: ctx.enter_context(nc.semaphore(name))
        wqkv = sb("wqkv_rows", [P, 12, D])
        wo = sb("wo_rows", [P, 4, D])
        wfc = sb("wfc_rows", [P, CF, D])
        wproj = sb("wproj_rows", [P, CD, F])
        t1 = sb("ternary_fc_rows", [P, CF, D], F16)
        t2 = sb("ternary_proj_rows", [P, CD, F], F16)
        id32 = keep["id32"]
        id16 = sb("id16", [P, P], F16)
        ones16 = sb("ones16", [P, P], F16)
        part = sb("per_partition", [P, 4])
        total = sb("over_partitions", [P, 4])
        thr = sb("thresholds", [P, 6])
        ps = ctx.enter_context(nc.psum_tensor("weight_psum", [P, 4, BANK], F32))
        ps16 = ctx.enter_context(nc.psum_tensor("weight_psum16", [P, 3, 2 * BANK], F16))
        psw = ctx.enter_context(nc.psum_tensor("colsum_psum", [P, BANK], F32))
        ld = {k: sem(f"loaded_{k}") for k in ("qkv", "fc", "o", "proj")}
        ident, parts, reduced, step = sem("ident"), sem("parts"), sem("reduced"), sem("vector_step")
        proj_part = sem("proj_part")
        scaled = sem("scaled")
        full32, hi_out, free32 = sem("full32"), sem("hi_out"), sem("free32")
        tern, full16, out16 = sem("ternary_ready"), sem("full16"), sem("out16")
        wo_full, wo_out = sem("wo_full"), sem("wo_out")
        cs_full, cs_out = sem("colsum_full"), sem("colsum_out")
        S = keep["scal"]
        block = ctx.enter_context(nc.Block())
        u32 = [(c, j) for c in range(CD) for j in range(THIRDS)]

        @block.sync
        def _(sp):
            sp.dma_start(wqkv[:], W_qkv.rearrange("(j p) d -> p j d", p=P)).then_inc(ld["qkv"], 16)
            sp.dma_start(wfc[:], w_fc.rearrange("(j p) d -> p j d", p=P)).then_inc(ld["fc"], 16)
            sp.dma_start(wproj[:], w_proj.rearrange("(j p) f -> p j f", p=P)).then_inc(ld["proj"], 16)
            sp.dma_start(wo[:], W_o.rearrange("(j p) d -> p j d", p=P)).then_inc(ld["o"], 16)

        @block.gpsimd
        def _(pool):
            nc.gpsimd.memset(id32[:], 0.0)
            nc.gpsimd.memset(id16[:], 0.0).then_inc(ident, 1)
            pool.wait_ge(ident, 1)
            for m in (id32, id16):
                nc.gpsimd.affine_select(out=m[:], in_=m[:], compare_op=ALU.not_equal, fill=1.0, base=0,
                                        pattern=[[-1, P]], channel_multiplier=1).then_inc(ident, 1)
            for k, value in enumerate((-0.5, EPS_LN, EPS_BIT)):
                nc.gpsimd.memset(keep["powers"][:, 4 * k:4 * k + 4], value)
            nc.gpsimd.memset(ones16[:], 1.0)
            nc.gpsimd.memset(keep["ones32"][:], 1.0).then_inc(ident, 1)
            for k, op in enumerate((bass.bass_isa.ReduceOp.max, bass.bass_isa.ReduceOp.add, bass.bass_isa.ReduceOp.add)):
                if k < 2:
                    pool.wait_ge(parts, k + 1)
                else:
                    pool.wait_ge(proj_part, 1)
                nc.gpsimd.partition_all_reduce(total[:, k:k + 1], part[:, k:k + 1], P, op).then_inc(reduced, 1)

        @block.vector
        def _(dve):
            count = [0]

            def link(ins):
                count[0] += 1
                ins.then_inc(step, 1)
                dve.wait_ge(step, count[0])

            dve.wait_ge(ld["qkv"], 16)
            nc.vector.tensor_reduce(part[:, 0:1], wqkv[:], axis=AX.XY, op=ALU.max,
                                    apply_absolute_value=True).then_inc(parts, 1)
            dve.wait_ge(reduced, 1)
            link(nc.vector.tensor_scalar(S["unscale"], total[:, 0:1], 1e-30, 1.0 / TOP, ALU.max, ALU.mult))
            nc.vector.reciprocal(S["scale"], S["unscale"]).then_inc(scaled, 1)
            dve.wait_ge(scaled, 1)

            def low_parts():
                for u, (c, j) in enumerate(u32):
                    dve.wait_ge(hi_out, u + 1)
                    cols = slice(j * BANK, (j + 1) * BANK)
                    nc.vector.scalar_tensor_tensor(keep["wl"][:, c, cols], ps[:, u % 4, :], S["scale"],
                                                   keep["wh"][:, c, cols], ALU.mult, ALU.subtract).then_inc(free32, 1)

            def ternary(k, name, rows, out, thr0, gamma):
                dve.wait_ge(ld[name], 16)
                flat = rows[:].rearrange("p a b -> p (a b)")
                if k == 1:
                    nc.vector.tensor_reduce(part[:, k:k + 1], rows[:], axis=AX.XY, op=ALU.add,
                                            apply_absolute_value=True).then_inc(parts, 1)
                dve.wait_ge(reduced, k + 1)
                link(nc.vector.tensor_scalar(gamma, total[:, k:k + 1], 1.0 / n_w, None, ALU.mult))
                link(nc.vector.tensor_scalar(thr[:, thr0:thr0 + 1], gamma, EPS_BIT, 0.5, ALU.add, ALU.mult))
                link(nc.vector.tensor_scalar(thr[:, thr0 + 1:thr0 + 2], thr[:, thr0:thr0 + 1], -1.0, None, ALU.mult))
                tern_rows = out[:].rearrange("p a b -> p (a b)")
                link(nc.vector.tensor_scalar(tern_rows, flat, thr[:, thr0 + 1:thr0 + 2], None, ALU.is_lt))
                nc.vector.scalar_tensor_tensor(tern_rows, flat, thr[:, thr0:thr0 + 1], tern_rows,
                                               ALU.is_gt, ALU.subtract).then_inc(tern, 1)
                dve.wait_ge(tern, k)

            low_parts()
            ternary(1, "fc", wfc, t1, 0, S["gamma1"])
            ternary(2, "proj", wproj, t2, 2, S["gamma2"])
            link(nc.vector.reciprocal(S["inv1"], S["gamma1"]))
            link(nc.vector.tensor_scalar(S["ninv1"], S["inv1"], -1.0, None, ALU.mult))
            nc.vector.tensor_tensor(S["gamma12"], S["gamma1"], S["gamma2"], ALU.mult)
            for c in range(CD):
                dve.wait_ge(wo_full, c + 1)
                nc.vector.tensor_copy(keep["woT"][:, c, :], ps[:, c, :]).then_inc(wo_out, 1)
            dve.wait_ge(cs_full, 1)
            nc.vector.tensor_copy(keep["colsum"][:], psw[:]).then_inc(cs_out, 1)

        @block.tensor
        def _(pe):
            pe.wait_ge(ident, 4)
            pe.wait_ge(ld["qkv"], 16)
            for u, (c, j) in enumerate(u32):
                wait(pe, free32, u - 3)
                for r in range(4):
                    last = nc.tensor.transpose(ps[:, u % 4, r * P:(r + 1) * P],
                                               wqkv[:, 4 * j + r, c * P:(c + 1) * P], id32[:])
                last.then_inc(full32, 1)

            def unit16(u, tiles):
                wait(pe, out16, u - 2)
                for r, tile in enumerate(tiles):
                    last = nc.tensor.transpose(ps16[:, u % 3, r * P:(r + 1) * P], tile, id16[:])
                last.then_inc(full16, 1)

            pe.wait_ge(tern, 1)
            for u in range(16):
                c, j = u % 4, u // 4
                unit16(u, [t1[:, 4 * j + r, c * P:(c + 1) * P] for r in range(4)])
            pe.wait_ge(tern, 2)
            for f in range(CF):
                unit16(16 + f, [t2[:, r, f * P:(f + 1) * P] for r in range(4)])
            pe.wait_ge(free32, len(u32))
            pe.wait_ge(ld["o"], 16)
            for c in range(CD):
                for r in range(4):
                    last = nc.tensor.transpose(ps[:, c, r * P:(r + 1) * P], wo[:, r, c * P:(c + 1) * P], id32[:])
                last.then_inc(wo_full, 1)
            pe.wait_ge(out16, 16 + CF)
            for f in range(CF):
                last = nc.tensor.matmul(psw[:], ones16[:], keep["t2T"][:, f, :], start=(f == 0), stop=(f == CF - 1))
            last.then_inc(cs_full, 1)

        @block.scalar
        def _(act):
            act.wait_ge(scaled, 1)
            for u, (c, j) in enumerate(u32):
                act.wait_ge(full32, u + 1)
                nc.scalar.activation(keep["wh"][:, c, j * BANK:(j + 1) * BANK], ps[:, u % 4, :], ACT.Copy,
                                     scale=S["scale"]).then_inc(hi_out, 1)
            act.wait_ge(ld["proj"], 16)
            nc.scalar.activation(t2[:], wproj[:], ACT.Abs, accum_out=part[:, 2:3]).then_inc(proj_part, 1)
            for u in range(16):
                c, j = u % 4, u // 4
                act.wait_ge(full16, u + 1)
                nc.scalar.copy(keep["t1T"][:, c, j * 4 * P:(j + 1) * 4 * P], ps16[:, u % 3, 0:4 * P]).then_inc(out16, 1)
            for f in range(CF):
                act.wait_ge(full16, 16 + f + 1)
                nc.scalar.copy(keep["t2T"][:, f, :], ps16[:, (16 + f) % 3, 0:4 * P]).then_inc(out16, 1)


def token_stage(nc, x, qkv_dram, yx_dram, keep):
    x_v = x.rearrange("(t p i) d -> t p i d", p=P, i=4)
    yx_v = yx_dram.rearrange("(t p i) d -> t p i d", p=P, i=4)
    qkv_v = qkv_dram.rearrange("(t p i) e -> t p i e", p=P, i=4)
    with ExitStack() as ctx:
        sb = lambda name, shape, dt=F32: ctx.enter_context(nc.sbuf_tensor(name, shape, dt))
        sem = lambda name: ctx.enter_context(nc.semaphore(name))
        xs = sb("x_rows", [P, 2, 4, D])
        x2 = sb("x_normed", [P, 4, D])
        xh = sb("x_hi", [P, 2, CD, TT], F16)
        xl = sb("x_lo", [P, 2, CD, TT], F16)
        g = sb("gelu_out", [P, 4, 2 * BANK])
        sq = sb("gelu_squared", [P, 2, 2 * BANK])
        gacc = sb("gelu_sum", [P, 2 * BANK])
        sqacc = sb("square_sum", [P, 2 * BANK])
        hh = sb("h_hi", [P, CF, TT], F16)
        hl = sb("h_lo", [P, CF, TT], F16)
        qkv = sb("qkv_rows", [P, 2, E3])
        cen = sb("centred", [P, D])
        bn = sb("bn", [P, 4, 6])
        mv = sb("mean_var", [P, 4, 2])
        sm = sb("norm_small", [P, 8, 4])
        rc = sb("qkv_scale", [P, 2, 4])
        st = sb("hidden_stats", [P, 8, 4])
        psA = ctx.enter_context(nc.psum_tensor("psA", [P, 4, BANK], F32))
        psB = ctx.enter_context(nc.psum_tensor("psB", [P, 2, BANK], F32))
        psC = ctx.enter_context(nc.psum_tensor("psC", [P, 2, BANK], F32))
        x_loaded = [sem("x_loaded0"), sem("x_loaded1")]
        y_stored = [sem("y_stored0"), sem("y_stored1")]
        qkv_stored = [sem("qkv_stored0"), sem("qkv_stored1")]
        bn_done, mv_ready, pool_step, norm_ready = sem("bn_done"), sem("mv_ready"), sem("pool_step"), sem("norm_ready")
        x2_ready, t_full, xh_ready, xl_ready = sem("x2_ready"), sem("t_full"), sem("xh_ready"), sem("xl_ready")
        a_full, g_ready, sq_ready = sem("a_full"), sem("g_ready"), sem("sq_ready")
        hh_ready, hl_ready = sem("hh_ready"), sem("hl_ready")
        g_added, sq_added = sem("g_added"), sem("sq_added")
        g_folded, sq_folded = sem("g_folded"), sem("sq_folded")
        b_full, b_out = sem("qkv_full"), sem("qkv_out")
        st_full, st_out, st_step, var_ready, rs_ready = sem("st_full"), sem("st_out"), sem("st_step"), sem("var_ready"), sem("rs_ready")
        y_full, cen_ready, y_ready = sem("y_full"), sem("cen_ready"), sem("y_ready")
        S = keep["scal"]
        block = ctx.enter_context(nc.Block())
        last_adds = UNITS1 - 1
        PS = 9
        VS = 6

        def steps(eng, body):
            body(0, 0, True)
            body(1, 1, True)
            with eng.Fori(1, STEPS // 2 - 1) as n:
                body((n, 2, 0), 0, True)
                body((n, 2, 1), 1, True)
            body(STEPS - 2, 0, True)
            body(STEPS - 1, 1, False)

        def turn(t, k):
            return k * (t // 2) if isinstance(t, int) else t[0] * k + (t[2] // 2) * k

        def at(t):
            return t if isinstance(t, int) else t[0] * t[1] + t[2]

        @block.sync
        def _(sp):
            sp.dma_start(xs[:, 0], x_v[0]).then_inc(x_loaded[0], 16)

            def body(t, s, has_next):
                if has_next:
                    nxt = shift(t, 1)
                    wait(sp, y_stored[1 - s], turn(nxt, 16))
                    sp.dma_start(xs[:, 1 - s], x_v[at(nxt)]).then_inc(x_loaded[1 - s], 16)
                for i in range(4):
                    sp.wait_ge(b_out, lin(t, 12, 3 * i + 3))
                    sp.dma_start(qkv_v[at(t)][:, i, :], qkv[:, i % 2, :]).then_inc(qkv_stored[i % 2], 16)
                sp.wait_ge(y_ready, lin(t, 4, 4))
                sp.dma_start(yx_v[at(t)], xs[:, s]).then_inc(y_stored[s], 16)

            steps(sp, body)
            for k in range(2):
                sp.wait_ge(y_stored[k], 16 * STEPS // 2)
                sp.wait_ge(qkv_stored[k], 16 * STEPS * 2)

        @block.gpsimd
        def _(pool):
            def norm(t, s):
                k = [0]

                def link(ins):
                    k[0] += 1
                    ins.then_inc(pool_step, 1)
                    pool.wait_ge(pool_step, lin(t, PS, k[0]))

                var = mv[:, :, 1]
                v1, r1, a, v2, v2e, r2 = (sm[:, j, :] for j in range(6))
                pool.wait_ge(mv_ready, lin(t, 1, 1))
                link(nc.gpsimd.tensor_tensor(v1, var, keep["powers"][:, 4:8], ALU.add))
                link(nc.gpsimd.tensor_tensor(r1, v1, keep["powers"][:, 0:4], ALU.pow))
                link(nc.gpsimd.tensor_tensor(a, var, r1, ALU.mult))
                link(nc.gpsimd.tensor_tensor(v2, a, r1, ALU.mult))
                link(nc.gpsimd.tensor_tensor(v2e, v2, keep["powers"][:, 8:12], ALU.add))
                link(nc.gpsimd.tensor_tensor(r2, v2e, keep["powers"][:, 0:4], ALU.pow))
                link(nc.gpsimd.tensor_tensor(sm[:, 6, :], r1, r2, ALU.mult))
                link(nc.gpsimd.tensor_tensor(a, v2e, r2, ALU.mult))
                link(nc.gpsimd.tensor_tensor(rc[:, s, :], a, S["unscale"].to_broadcast([P, 4]), ALU.mult))

            def body(t, s, has_next):
                for j in range(1, UNITS1):
                    pool.wait_ge(g_ready, lin(t, UNITS1, j + 1))
                    if j == 1:
                        wait(pool, st_full, lin(t, 1))
                    else:
                        pool.wait_ge(g_added, lin(t, last_adds, j - 1))
                    nc.gpsimd.tensor_tensor(gacc[:], g[:, 0, :] if j == 1 else gacc[:], g[:, j % 4, :],
                                            ALU.add).then_inc(g_added, 1)
                pool.wait_ge(g_added, lin(t, last_adds, last_adds))
                nc.gpsimd.tensor_tensor(gacc[:, 0:BANK], gacc[:, 0:BANK], gacc[:, BANK:2 * BANK], ALU.add).then_inc(g_folded, 1)
                if has_next:
                    norm(shift(t, 1), 1 - s)
                pool.wait_ge(var_ready, lin(t, 1, 1))
                nc.gpsimd.tensor_tensor(st[:, 5, :], st[:, 4, :], keep["powers"][:, 0:4], ALU.pow).then_inc(rs_ready, 1)

            norm(0, 0)
            steps(pool, body)

        @block.vector
        def _(dve):
            def stats(t, s):
                dve.wait_ge(x_loaded[s], turn(t, 16) + 16)
                for i in range(4):
                    last = nc.vector.bn_stats(bn[:, i, :], xs[:, s, i, :])
                last.then_inc(bn_done, 1)
                dve.wait_ge(bn_done, lin(t, 1, 1))
                nc.vector.memset(sm[:, 7, 0:1], 0.0)
                for i in range(4):
                    last = nc.vector.bn_aggr(mv[:, i, :], bn[:, i, :])
                last.then_inc(mv_ready, 1)

            def normed(t, s):
                dve.wait_ge(pool_step, lin(t, PS, PS))
                dve.wait_ge(mv_ready, lin(t, 1, 1))
                wait(dve, t_full, lin(t, 4))
                for i in range(4):
                    last = nc.vector.tensor_scalar(x2[:, i, :], xs[:, s, i, :], mv[:, i, 0:1], sm[:, 6, i:i + 1],
                                                   ALU.subtract, ALU.mult)
                last.then_inc(x2_ready, 1)

            def low(t, s):
                for c in range(CD):
                    dve.wait_ge(xh_ready, lin(t, 4, c + 1))
                    nc.vector.tensor_tensor(xl[:, s, c, :], psC[:, (1 - s + c) % 2, :], xh[:, s, c, :],
                                            ALU.subtract).then_inc(xl_ready, 1)

            def add_square(t, j):
                dve.wait_ge(sq_ready, lin(t, UNITS1, j + 1))
                if j == 1:
                    wait(dve, st_full, lin(t, 1))
                else:
                    dve.wait_ge(sq_added, lin(t, last_adds, j - 1))
                nc.vector.tensor_tensor(sqacc[:], sq[:, 0, :] if j == 1 else sqacc[:], sq[:, j % 2, :],
                                        ALU.add).then_inc(sq_added, 1)

            def fold_squares(t):
                dve.wait_ge(sq_added, lin(t, last_adds, last_adds))
                nc.vector.tensor_tensor(sqacc[:, 0:BANK], sqacc[:, 0:BANK], sqacc[:, BANK:2 * BANK],
                                        ALU.add).then_inc(sq_folded, 1)

            def body(t, s, has_next):
                wait(dve, y_full, lin(t, 4))
                for j in range(UNITS1):
                    dve.wait_ge(g_ready, lin(t, UNITS1, j + 1))
                    pair = slice(2 * j, 2 * j + 2)
                    gj = g[:, j % 4, :].rearrange("p (a b) -> p a b", a=2)
                    nc.vector.tensor_scalar(hh[:, pair, :], gj, S["inv1"], None, ALU.mult).then_inc(hh_ready, 1)
                    if j >= 2:
                        add_square(t, j - 1)
                    dve.wait_ge(hh_ready, lin(t, UNITS1, j + 1))
                    nc.vector.scalar_tensor_tensor(hl[:, pair, :], gj, S["inv1"], hh[:, pair, :],
                                                   ALU.mult, ALU.subtract).then_inc(hl_ready, 1)
                if has_next:
                    stats(shift(t, 1), 1 - s)
                add_square(t, UNITS1 - 1)
                fold_squares(t)
                if has_next:
                    normed(shift(t, 1), 1 - s)
                    low(shift(t, 1), 1 - s)

                k = [0]

                def link(ins):
                    k[0] += 1
                    ins.then_inc(st_step, 1)
                    dve.wait_ge(st_step, lin(t, VS, k[0]))

                dve.wait_ge(st_full, lin(t, 1, 1))
                nc.vector.tensor_scalar(st[:, 0:2, :], psC[:, (s + 4) % 2, 0:8].rearrange("p (a b) -> p a b", a=2),
                                        1.0 / F, None, ALU.mult).then_inc(st_out, 1)
                dve.wait_ge(st_out, lin(t, 1, 1))
                mean, ms, var, var_eps, rs, rv, ratio = (st[:, j, :] for j in (0, 1, 2, 4, 5, 3, 6))
                link(nc.vector.tensor_tensor(var, mean, mean, ALU.mult))
                link(nc.vector.tensor_tensor(var, ms, var, ALU.subtract))
                link(nc.vector.tensor_scalar(var, var, 0.0, None, ALU.max))
                nc.vector.tensor_scalar(var_eps, var, EPS_BIT, None, ALU.add).then_inc(var_ready, 1)
                link(nc.vector.reciprocal(rv, var))
                nc.vector.tensor_scalar(mean, mean, S["ninv1"], None, ALU.mult)
                link(nc.vector.tensor_tensor(ratio, var, rv, ALU.mult))
                dve.wait_ge(rs_ready, lin(t, 1, 1))
                link(nc.vector.scalar_tensor_tensor(st[:, 7, :], rs, S["gamma12"], ratio, ALU.mult, ALU.mult))
                for i in range(4):
                    dve.wait_ge(y_full, lin(t, 4, i + 1))
                    if i:
                        dve.wait_ge(y_ready, lin(t, 4, i))
                    else:
                        wait(dve, y_ready, lin(t, 4))
                    nc.vector.scalar_tensor_tensor(cen[:], keep["colsum"][:], st[:, 0, i:i + 1],
                                                   psC[:, (s + 5 + i) % 2, :], ALU.mult, ALU.add).then_inc(cen_ready, 1)
                    dve.wait_ge(cen_ready, lin(t, 4, i + 1))
                    nc.vector.scalar_tensor_tensor(xs[:, s, i, :], cen[:], st[:, 7, i:i + 1], xs[:, s, i, :],
                                                   ALU.mult, ALU.add).then_inc(y_ready, 1)

            stats(0, 0)
            normed(0, 0)
            low(0, 0)
            steps(dve, body)

        @block.scalar
        def _(act):
            def high(t, s, chunks):
                for c in chunks:
                    act.wait_ge(t_full, lin(t, 4, c + 1))
                    nc.scalar.copy(xh[:, s, c, :], psC[:, (1 - s + c) % 2, :]).then_inc(xh_ready, 1)

            def square(t, j):
                act.wait_ge(g_ready, lin(t, UNITS1, j + 1))
                if j >= 2:
                    act.wait_ge(sq_added, lin(t, last_adds, max(j - 2, 1)))
                else:
                    wait(act, sq_added, lin(t, last_adds))
                nc.scalar.activation(sq[:, j % 2, :], g[:, j % 4, :], ACT.Square).then_inc(sq_ready, 1)

            def body(t, s, has_next):
                for j in range(UNITS1):
                    act.wait_ge(a_full, lin(t, UNITS1, j + 1))
                    if j >= 4:
                        act.wait_ge(hl_ready, lin(t, UNITS1, j - 3))
                        act.wait_ge(g_added, lin(t, last_adds, max(j - 4, 1)))
                    else:
                        wait(act, hl_ready, lin(t, UNITS1, j - 3))
                        wait(act, g_added, lin(t, last_adds, j - 3))
                    nc.scalar.activation(g[:, j % 4, :], psA[:, 2 * (j % 2):2 * (j % 2) + 2, :], ACT.Gelu,
                                         scale=S["gamma1"]).then_inc(g_ready, 1)
                    if j:
                        square(t, j - 1)
                square(t, UNITS1 - 1)
                for u in range(12):
                    i, third = divmod(u, THIRDS)
                    if u in (8, 10) and has_next:
                        high(shift(t, 1), 1 - s, (u - 8, u - 7))
                    act.wait_ge(b_full, lin(t, 12, u + 1))
                    if third == 0:
                        wait(act, qkv_stored[i % 2], lin(t, 32, 16 * (i // 2)))
                    act.wait_ge(pool_step, lin(t, PS, PS))
                    nc.scalar.activation(qkv[:, i % 2, third * BANK:(third + 1) * BANK], psB[:, u % 2, :], ACT.Copy,
                                         scale=rc[:, s, i:i + 1]).then_inc(b_out, 1)

            high(0, 0, range(CD))
            steps(act, body)

        @block.tensor
        def _(pe):
            def transposes(t, s, chunks, first=False):
                pe.wait_ge(x2_ready, lin(t, 1, 1))
                for c in chunks:
                    if c >= 2:
                        pe.wait_ge(xl_ready, lin(t, 4, c - 1))
                    elif not first:
                        wait(pe, cen_ready, lin(t, 4, c - 5))
                    for i in range(4):
                        last = nc.tensor.transpose(psC[:, (1 - s + c) % 2, i * P:(i + 1) * P],
                                                   x2[:, i, c * P:(c + 1) * P], keep["id32"][:])
                    last.then_inc(t_full, 1)

            def body(t, s, has_next):
                pe.wait_ge(xl_ready, lin(t, 4, 4))
                for j in range(UNITS1):
                    wait(pe, g_ready, lin(t, UNITS1, j - 1))
                    for b in range(2):
                        f = 2 * j + b
                        for c in range(CD):
                            w = keep["t1T"][:, c, f * P:(f + 1) * P]
                            for k, xx in enumerate((xh, xl)):
                                last = nc.tensor.matmul(psA[:, 2 * (j % 2) + b, :], w, xx[:, s, c, :],
                                                        start=(c == 0 and k == 0), stop=(c == CD - 1 and k == 1))
                    last.then_inc(a_full, 1)
                for u in range(12):
                    i, third = divmod(u, THIRDS)
                    if u in (8, 10) and has_next:
                        transposes(shift(t, 1), 1 - s, (u - 8, u - 7))
                    wait(pe, b_out, lin(t, 12, u - 1))
                    cols = slice(third * BANK, (third + 1) * BANK)
                    terms = [(xx, ww, c) for c in range(CD) for xx, ww in ((xh, "wh"), (xh, "wl"), (xl, "wh"))]
                    for k, (xx, ww, c) in enumerate(terms):
                        last = nc.tensor.matmul(psB[:, u % 2, :], xx[:, s, c, i * P:(i + 1) * P], keep[ww][:, c, cols],
                                                start=(k == 0), stop=(k == len(terms) - 1))
                    last.then_inc(b_full, 1)
                pe.wait_ge(g_folded, lin(t, 1, 1))
                pe.wait_ge(sq_folded, lin(t, 1, 1))
                if has_next:
                    pe.wait_ge(xl_ready, lin(t, 4, 8))
                else:
                    pe.wait_ge(cen_ready, lin(t, 4))
                for q, acc in enumerate((gacc, sqacc)):
                    for i in range(4):
                        last = nc.tensor.matmul(psC[:, (s + 4) % 2, 4 * q + i:4 * q + i + 1],
                                                acc[:, i * P:(i + 1) * P], keep["ones32"][:, 0:1], start=True, stop=True)
                last.then_inc(st_full, 1)
                pe.wait_ge(hl_ready, lin(t, UNITS1, UNITS1))
                for i in range(4):
                    if i == 1:
                        pe.wait_ge(st_out, lin(t, 1, 1))
                    elif i >= 2:
                        pe.wait_ge(cen_ready, lin(t, 4, i - 1))
                    for f in range(CF):
                        for k, h in enumerate((hh, hl)):
                            last = nc.tensor.matmul(psC[:, (s + 5 + i) % 2, :], h[:, f, i * P:(i + 1) * P],
                                                    keep["t2T"][:, f, :], start=(f == 0 and k == 0),
                                                    stop=(f == CF - 1 and k == 1))
                    last.then_inc(y_full, 1)

            transposes(0, 0, range(CD), first=True)
            steps(pe, body)


DEN_STEPS = KT_N - POOLED + 1
MISC = {0: {1: ("T", 1, 0, 3), 7: ("T", 1, 1, 0)}, 1: {1: ("T", 1, 1, 1), 7: ("T", 1, 1, 2)},
        2: {1: ("T", 1, 1, 3), 5: ("D", 1, 1, 0)}, 3: {5: ("D", 1, 1, 1)}, 4: {5: ("D", 1, 1, 2)},
        5: {1: ("A", 0), 7: ("T", 1, 2, 0)}, 6: {1: ("T", 1, 2, 1), 7: ("T", 1, 2, 2)},
        7: {1: ("T", 1, 2, 3), 7: ("T", 1, 3, 0)}, 8: {3: ("A", 1), 7: ("T", 1, 3, 1)},
        9: {1: ("T", 1, 3, 2), 7: ("T", 1, 3, 3)},
        10: {5: ("D", 0, 0, 0)}, 11: {5: ("D", 0, 0, 1)}, 12: {5: ("D", 0, 0, 2)},
        13: {1: ("A", 2), 7: ("T", 2, 0, 0)}, 14: {1: ("T", 2, 0, 1)}, 15: {3: ("A", 3), 7: ("T", 2, 0, 2)}}
MAXIMA = [(0, 1, 2, 4, 7), (0, 1, 2, 4, 7), (0, 2, 4, 5), (0, 2, 4, 5), (0, 2, 4, 5), (0, 1, 2, 4, 7), (0, 2, 4, 7),
          (0, 1, 2, 4, 7), (0, 2, 4, 7), (0, 1, 2, 4, 7), (0, 2, 4, 5), (0, 2, 4, 5), (0, 2, 4, 5), (0, 2, 4, 7),
          (0, 1, 2), ()]
BUILD = {1: (1, 2), 4: (1, 3), 8: (2, 0), 10: (2, 1)}
COLLECT = {5: (1, 1), 13: (0, 0)}
INVERT = {6: (1, 1), 14: (0, 0)}
SPREAD = {7: (1, 1), 15: (0, 0)}
NORMALISE = {1: (1, 0), 8: (1, 1)}
STORE = {2: (1, 0), 9: (1, 1)}


def attention_stage(nc, qkv_dram, ot_dram, den_dram, keep):
    per_head = 2 * KT_N
    scale = DH ** -0.5
    blocks = qkv_dram.rearrange("t e -> (t e)").rearrange("(m h p x) -> m p h x", h=HG, p=P, x=HEAD // P)
    with ExitStack() as ctx:
        sb = lambda name, shape, dt=F32: ctx.enter_context(nc.sbuf_tensor(name, shape, dt))
        sem = lambda name: ctx.enter_context(nc.semaphore(name))
        qn = sb("q_rows", [P, HG, KT_N, DH])
        kn = sb("k_rows", [P, HG, KT_N, DH])
        v = sb("v_rows", [P, 2, HG, KT_N, DH])
        qs = sb("q_stack", [P, 2, KT_N, 3, DH])
        ks = sb("k_stack", [P, 2, KT_N, 3, DH])
        qT = sb("q_stackT", [P, 2, HG, L], F32R)
        kT = sb("k_stackT", [P, 2, HG, L], F32R)
        pr = sb("probs", [P, 8, HG, BANK])
        acc = sb("probs_sum", [P, 2, HG, BANK])
        oraw = sb("out_raw", [P, 2, BANK])
        den = sb("denominators", [P, BANK])
        few = sb("denominators_once", [P, 2, HG * BANK // P])
        rfew = sb("inverses_once", [P, 2, HG * BANK // P])
        rden = sb("inverse_denominators", [P, 2, BANK])
        on = sb("out_normed", [P, 2, BANK])
        mx = sb("half_maxima", [P, HG, KT_N, 2])
        nm = sb("negated_maxima", [P, 2, KT_N])
        au = sb("maxima_parts", [P, 2, 2, KT_N])
        rows = sb("maxima_rows", [2 * KT_N, 2, P])
        id32r = sb("id32r", [P, P], F32R)
        psX = ctx.enter_context(nc.psum_tensor("scores_for_maxima", [P, 2, BANK], F32))
        psS = ctx.enter_context(nc.psum_tensor("scores", [P, 2, 2, BANK], F32))
        psO = ctx.enter_context(nc.psum_tensor("outputs", [P, BANK], F32))
        psM = ctx.enter_context(nc.psum_tensor("misc", [P, BANK], F32))
        qk_loaded, v_loaded = sem("qk_loaded"), [sem("v_loaded0"), sem("v_loaded1")]
        ones_set = sem("ones_set")
        hi_ready, lo_ready = sem("hi_ready"), sem("lo_ready")
        t_full, t_out = sem("stacks_transposed"), sem("stacksT_ready")
        x_full, max_done, aug_step = sem("max_scores_full"), sem("max_done"), sem("maxima_step")
        a_full, rows_ready = sem("maxima_transposed"), sem("maxima_rows_ready")
        aug_loaded = [sem(f"maxima_loaded{h}") for h in range(HG)]
        s_full, exp_done, pv_done = sem("scores_full"), sem("exp_done"), sem("pv_done")
        added = sem("probs_added")
        den_stored, few_loaded, inverted = sem("den_stored"), sem("few_loaded"), sem("inverted")
        inv_stored, inv_loaded = sem("inverses_stored"), sem("inverses_loaded")
        d_full, d_out, oraw_out, on_ready = sem("den_full"), sem("den_out"), sem("out_raw_ready"), sem("out_normed_ready")
        ot_stored = [sem("ot_stored0"), sem("ot_stored1")]
        block = ctx.enter_context(nc.Block())

        def slot(g):
            return g % 2 if isinstance(g, int) else g[2] % 2

        def turn(g, k):
            return k * (g // 2) if isinstance(g, int) else g[0] * k + (g[2] // 2) * k

        def at(g):
            return g if isinstance(g, int) else g[0] * g[1] + g[2]

        def groups(eng, body):
            body(-1, False, True)
            body(0, True, True)
            with eng.Fori(0, (GROUPS - 4) // 2) as m:
                body((m, 2, 1), True, True)
                body((m, 2, 2), True, True)
            body(GROUPS - 3, True, True)
            body(GROUPS - 2, True, True)
            body(GROUPS - 1, True, False)

        def builds(g, w, nxt):
            ahead, h = BUILD.get(w, (0, 0))
            last = isinstance(g, int) and g + ahead >= GROUPS
            return (shift(g, ahead), h) if ahead and nxt and not last else None

        def has_half(g, cur, back):
            return cur and not (back and isinstance(g, int) and g == 0)

        def half(table, g, w, cur):
            back, hf = table.get(w, (0, 0))
            return (shift(g, -back), hf) if w in table and has_half(g, cur, back) else None

        def misc(g, w, cur, nxt):
            def has(e):
                if e[0] == "D":
                    return has_half(g, cur, e[1])
                return nxt and not (e[0] == "T" and isinstance(g, int) and g + e[1] >= GROUPS)
            return {k: e for k, e in MISC.get(w, {}).items() if has(e)}

        def maxima(w, nxt):
            begin = sum(len(m) for m in MAXIMA[:w])
            return range(begin, begin + (len(MAXIMA[w]) if nxt else 0))

        def freed(g, e):
            if e[0] == "T":
                return t_out, lin(shift(g, e[1]), 4 * HG, 4 * e[2] + e[3] + 1)
            if e[0] == "A":
                return rows_ready, lin(shift(g, 1), HG, e[1] + 1)
            return d_out, lin(shift(g, -e[1]), 2, e[2] + 1)

        @block.sync
        def _(sp):
            def load_block(dst, g, section):
                group = at(g)
                return sp.dma_start(dst.rearrange("p h i d -> p h (i d)"), blocks[group + (group // 4) * 8 + 4 * section])

            def load_qk(g):
                wait(sp, lo_ready, lin(g, 2 * HG))
                load_block(qn[:], g, 0).then_inc(qk_loaded, 16)
                load_block(kn[:], g, 1).then_inc(qk_loaded, 16)

            def load_maxima(g, h):
                sp.wait_ge(rows_ready, lin(g, HG, h + 1))
                sp.dma_start(qT[STACK:AUG, slot(g), h, :].bitcast(F32).rearrange("a (i c) -> a i c", c=P),
                             rows[:, h % 2, :]).then_inc(aug_loaded[h], 16)

            def collect(g, hf):
                sp.wait_ge(d_out, lin(g, 2, hf + 1))
                sp.dma_start(den_dram[0][hf], den[0:P:P // HG, :]).then_inc(den_stored, 16)
                sp.wait_ge(den_stored, lin(g, 32, 16 * hf + 16))
                sp.dma_start(few[:, hf, :], den_dram[0][hf].rearrange("h (a x) -> (h a) x", a=P // HG)).then_inc(few_loaded, 16)

            def spread(g, hf):
                sp.wait_ge(inverted, lin(g, 2, hf + 1))
                sp.dma_start(den_dram[1][hf].rearrange("h (a x) -> (h a) x", a=P // HG), rfew[:, hf, :]).then_inc(inv_stored, 16)
                sp.wait_ge(inv_stored, lin(g, 32, 16 * hf + 16))
                for h in range(HG):
                    sp.dma_start(rden[32 * h:32 * h + 32, hf, :],
                                 den_dram[1][hf][h:h + 1, :].to_broadcast([32, BANK])).then_inc(inv_loaded, 16)

            def store_ot(g, hf):
                sp.wait_ge(on_ready, lin(g, 2, hf + 1))
                sp.dma_start(ot_dram[at(g)][hf], on[:, hf, :]).then_inc(ot_stored[hf], 16)

            def body(g, cur, nxt):
                n = shift(g, 1)
                if nxt:
                    wait(sp, pv_done, lin(g, UNITS))
                    load_block(v[:, slot(n)], n, 2).then_inc(v_loaded[slot(n)], 16)
                for w in range(UNITS):
                    for e in misc(g, w, cur, nxt).values():
                        if e[0] == "A":
                            load_maxima(n, e[1])
                    if half(STORE, g, w, cur):
                        store_ot(*half(STORE, g, w, cur))
                    if half(COLLECT, g, w, cur):
                        collect(*half(COLLECT, g, w, cur))
                    if half(SPREAD, g, w, cur):
                        spread(*half(SPREAD, g, w, cur))
                    if w == 5 and nxt and not (isinstance(g, int) and g == GROUPS - 2):
                        load_qk(shift(g, 2))

            load_qk(0)
            groups(sp, body)
            store_ot(GROUPS - 1, 0)
            collect(GROUPS - 1, 1)
            spread(GROUPS - 1, 1)
            store_ot(GROUPS - 1, 1)
            for hf in range(2):
                sp.wait_ge(ot_stored[hf], 16 * GROUPS)

        @block.gpsimd
        def _(pool):
            def build(g, h):
                for k, (src, dst, hi, lo) in enumerate(((kn, ks, 0, 1), (qn, qs, 0, 2))):
                    pool.wait_ge(hi_ready, lin(g, 2 * HG, 2 * h + k + 1))
                    nc.gpsimd.tensor_tensor(dst[:, h % 2].bitcast(F32R)[:, :, lo, :], src[:, h], dst[:, h % 2, :, hi, :],
                                            ALU.subtract).then_inc(lo_ready, 1)

            def add(g, hf, j):
                if j == 1:
                    wait(pool, d_full, lin(g, 2, hf - 1))
                pool.wait_ge(exp_done, lin(g, 2 * UNITS, 2 * (8 * hf + j) + 2))
                if j > 1:
                    pool.wait_ge(added, lin(g, 2 * (POOLED - 1), (POOLED - 1) * hf + j - 1))
                nc.gpsimd.tensor_tensor(acc[:, hf], pr[:, 0] if j == 1 else acc[:, hf], pr[:, j],
                                        ALU.add).then_inc(added, 1)

            def normalise(g, hf):
                pool.wait_ge(inv_loaded, lin(g, 128, 64 * hf + 64))
                pool.wait_ge(oraw_out, lin(g, 2, hf + 1))
                wait(pool, ot_stored[hf], lin(g, 16))
                nc.gpsimd.tensor_tensor(on[:, hf, :], oraw[:, hf, :], rden[:, hf, :], ALU.mult).then_inc(on_ready, 1)

            def body(g, cur, nxt):
                for w in range(UNITS):
                    if cur and 1 <= w % 8 < POOLED:
                        add(g, w // 8, w % 8)
                    if builds(g, w, nxt):
                        build(*builds(g, w, nxt))
                    if half(NORMALISE, g, w, cur):
                        normalise(*half(NORMALISE, g, w, cur))

            build(0, 0)
            build(0, 1)
            groups(pool, body)
            for hf in range(2):
                normalise(GROUPS - 1, hf)

        @block.scalar
        def _(act):
            def build(g, h):
                act.wait_ge(qk_loaded, lin(g, 32, 32))
                wait(act, t_full, lin(g, 4 * HG, 4 * h - 4))
                for src, dst, step in ((kn, ks, 2), (qn, qs, 1)):
                    hi = dst[:, h % 2].bitcast(F32R)[:, :, 0:step + 1:step, :]
                    nc.scalar.copy(hi, src[:, h].unsqueeze(2).to_broadcast([P, KT_N, 2, DH])).then_inc(hi_ready, 1)

            def exp(g, w, hp):
                act.wait_ge(s_full, lin(g, 2 * UNITS, 2 * w + hp + 1))
                if hp == 0:
                    j, q = w % 8, w // 8 - 1
                    wait(act, pv_done, lin(g, UNITS, w - 7))
                    if j < POOLED:
                        wait(act, added, lin(g, 2 * (POOLED - 1), (POOLED - 1) * q + max(j, 1)))
                    else:
                        wait(act, d_full, lin(g, 2, q + 1))
                nc.scalar.activation(pr[:, w % 8, 2 * hp:2 * hp + 2, :], psS[:, hp], ACT.Exp,
                                     scale=scale).then_inc(exp_done, 1)

            def evacuate(g, h, q):
                act.wait_ge(t_full, lin(g, 4 * HG, 4 * h + q + 1))
                dst = (kT, qT)[q % 2]
                nc.scalar.copy(dst[0:STACK, slot(g), h, (q // 2) * BANK:(q // 2 + 1) * BANK],
                               psM[0:STACK, :]).then_inc(t_out, 1)

            def out_raw(g, hf):
                act.wait_ge(pv_done, lin(g, UNITS, 8 * hf + 8))
                wait(act, on_ready, lin(g, 2, hf - 1))
                nc.scalar.copy(oraw[:, hf, :], psO[:]).then_inc(oraw_out, 1)

            def denominators(g, hf):
                act.wait_ge(d_full, lin(g, 2, hf + 1))
                wait(act, den_stored, lin(g, 32, 16 * hf))
                nc.scalar.copy(den[:], psM[:]).then_inc(d_out, 1)

            def body(g, cur, nxt):
                for w in range(UNITS):
                    entries = misc(g, w, cur, nxt)
                    if cur:
                        exp(g, w, 0)
                    if 1 in entries and entries[1][0] == "T":
                        evacuate(shift(g, entries[1][1]), *entries[1][2:])
                    if cur:
                        exp(g, w, 1)
                    if cur and w == 0 and not (isinstance(g, int) and g == 0):
                        out_raw(shift(g, -1), 1)
                    if cur and w == 8:
                        out_raw(g, 0)
                    if 7 in entries and entries[7][0] == "T":
                        evacuate(shift(g, entries[7][1]), *entries[7][2:])
                    if 5 in entries and entries[5][0] == "D" and entries[5][3] == DEN_STEPS - 1:
                        denominators(shift(g, -entries[5][1]), entries[5][2])
                    if builds(g, w, nxt):
                        build(*builds(g, w, nxt))

            build(0, 0)
            build(0, 1)
            for q in range(3):
                evacuate(0, 0, q)
            groups(act, body)
            out_raw(GROUPS - 1, 1)
            denominators(GROUPS - 1, 1)

        @block.vector
        def _(dve):
            def maximum(g, r):
                dve.wait_ge(x_full, lin(g, per_head * HG, r + 1))
                h, t, kh = r // per_head, r % per_head // 2, r % 2
                nc.vector.tensor_reduce(mx[:, h, t, kh:kh + 1], psX[:, r % 2, :], axis=AX.X, op=ALU.max).then_inc(max_done, 1)

            def split_maxima(g, h, step):
                if step == 0:
                    dve.wait_ge(max_done, lin(g, per_head * HG, per_head * (h + 1)))
                    wait(dve, a_full, lin(g, HG, h - 1))
                    nc.vector.tensor_reduce(nm[:, h % 2, :], mx[:, h], axis=AX.X, op=ALU.max, negate=True).then_inc(aug_step, 1)
                elif step == 1:
                    dve.wait_ge(aug_step, lin(g, 3 * HG, 3 * h + 1))
                    nc.vector.tensor_copy(au[:, h % 2, 0, :].bitcast(F32R), nm[:, h % 2, :]).then_inc(aug_step, 1)
                else:
                    dve.wait_ge(aug_step, lin(g, 3 * HG, 3 * h + 2))
                    nc.vector.tensor_tensor(au[:, h % 2, 1, :].bitcast(F32R), nm[:, h % 2, :], au[:, h % 2, 0, :],
                                            ALU.subtract).then_inc(aug_step, 1)

            def copy_rows(g, h):
                dve.wait_ge(a_full, lin(g, HG, h + 1))
                wait(dve, aug_loaded[h % 2 + 2 * (1 - h // 2)], lin(g, 16, 16 * (h // 2)))
                nc.vector.tensor_copy(rows[:, h % 2, :], psM[0:2 * KT_N, 0:P]).then_inc(rows_ready, 1)

            def invert(g, hf):
                dve.wait_ge(few_loaded, lin(g, 32, 16 * hf + 16))
                wait(dve, inv_stored, lin(g, 32, 16 * hf - 16))
                nc.vector.reciprocal(rfew[:, hf, :], few[:, hf, :]).then_inc(inverted, 1)

            def body(g, cur, nxt):
                n = shift(g, 1)
                for w in range(UNITS):
                    entries = misc(g, w, cur, nxt)
                    for r in maxima(w, nxt):
                        maximum(n, r)
                        h, step = divmod(r, per_head)
                        if h and step < 3:
                            split_maxima(n, h - 1, step)
                        if r == maxima(w, nxt)[1]:
                            for e in (e for e in entries.values() if e[0] == "A"):
                                copy_rows(n, e[1])
                        if r == per_head * HG - 1:
                            for step in range(3):
                                split_maxima(n, HG - 1, step)
                    if 3 in entries and not MAXIMA[w]:
                        copy_rows(n, entries[3][1])
                    if half(INVERT, g, w, cur):
                        invert(*half(INVERT, g, w, cur))

            nc.vector.memset(kT[STACK:AUG, :, :, :].bitcast(F32), 1.0)
            nc.vector.tensor_copy(id32r[:], keep["id32"][:]).then_inc(ones_set, 1)
            groups(dve, body)
            invert(GROUPS - 1, 1)

        @block.tensor
        def _(pe):
            def scores(g, w, hp):
                hf, i = divmod(w, KT_N)
                wait(pe, exp_done, lin(g, 2 * UNITS, 2 * w + hp - 1))
                if w == 0:
                    if hp == 0:
                        pe.wait_ge(t_out, lin(g, 4 * HG, 4 * HG))
                    for h in (2 * hp, 2 * hp + 1):
                        pe.wait_ge(aug_loaded[h], lin(g, 16, 16))
                for k in range(2):
                    h = 2 * hp + k
                    last = nc.tensor.matmul(psS[:, hp, k, :], kT[0:AUG, slot(g), h, i * P:(i + 1) * P],
                                            qT[0:AUG, slot(g), h, hf * BANK:(hf + 1) * BANK], start=True, stop=True)
                last.then_inc(s_full, 1)

            def outputs(g, w):
                hf, i = divmod(w, KT_N)
                pe.wait_ge(exp_done, lin(g, 2 * UNITS, 2 * w + 2))
                if w == 0:
                    pe.wait_ge(v_loaded[slot(g)], turn(g, 16) + 16)
                if i == 0:
                    wait(pe, oraw_out, lin(g, 2, hf))
                for h in range(HG):
                    last = nc.tensor.matmul(psO[32 * h:32 * h + 32, :], v[:, slot(g), h, i, :], pr[:, w % 8, h, :],
                                            start=(i == 0), stop=(i == KT_N - 1))
                last.then_inc(pv_done, 1)

            def max_scores(g, r):
                h, t, kh = r // per_head, r % per_head // 2, r % 2
                if r % KT_N == 0:
                    pe.wait_ge(t_out, lin(g, 4 * HG, 4 * h + 3 + t // 4))
                wait(pe, max_done, lin(g, per_head * HG, r - 1))
                nc.tensor.matmul(psX[:, r % 2, :], qT[0:STACK, slot(g), h, t * P:(t + 1) * P],
                                 kT[0:STACK, slot(g), h, kh * BANK:(kh + 1) * BANK], start=True, stop=True).then_inc(x_full, 1)

            def transposes(g, h, q):
                pe.wait_ge(lo_ready, lin(g, 2 * HG, 2 * h + q % 2 + 1))
                src = (ks, qs)[q % 2][:, h % 2].bitcast(F32R).rearrange("p i r d -> p i (r d)")
                for k in range(4):
                    last = nc.tensor.transpose(psM[0:STACK, k * P:(k + 1) * P].bitcast(F32R), src[:, 4 * (q // 2) + k, :], id32r[:])
                last.then_inc(t_full, 1)

            def maxima_rows(g, h):
                pe.wait_ge(aug_step, lin(g, 3 * HG, 3 * h + 3))
                nc.tensor.transpose(psM[0:2 * KT_N, 0:P], au[:, h % 2].rearrange("p a i -> p (a i)"),
                                    keep["id32"][:]).then_inc(a_full, 1)

            def denominators(g, hf, k):
                if k == 0:
                    pe.wait_ge(exp_done, lin(g, 2 * UNITS, UNITS * (hf + 1)))
                part = pr[:, POOLED + k] if k < DEN_STEPS - 1 else acc[:, hf]
                if k == DEN_STEPS - 1:
                    pe.wait_ge(added, lin(g, 2 * (POOLED - 1), (POOLED - 1) * (hf + 1)))
                for h in range(HG):
                    last = nc.tensor.matmul(psM[32 * h:32 * h + 32, :], keep["ones32"][:, 0:32], part[:, h, :],
                                            start=(k == 0), stop=(k == DEN_STEPS - 1))
                if k == DEN_STEPS - 1:
                    last.then_inc(d_full, 1)

            def entry(g, e, before):
                if before and not (e[0] == "D" and e[3]):
                    wait(pe, *before)
                if e[0] == "T":
                    transposes(shift(g, e[1]), *e[2:])
                elif e[0] == "A":
                    maxima_rows(shift(g, 1), e[1])
                else:
                    denominators(shift(g, -e[1]), *e[2:])
                return freed(g, e)

            def body(g, cur, nxt):
                n = shift(g, 1)
                first = isinstance(g, int) and g == 0
                before = freed(shift(g, -1), ("T", 2, 0, 2) if nxt else ("A", 3))
                for w in range(UNITS):
                    entries = misc(g, w, cur, nxt)
                    prev = (g, w - 1) if w else (shift(g, -1), UNITS - 1)
                    for k in range(8):
                        if k in entries:
                            before = entry(g, entries[k], before)
                        elif cur and k in (0, 2):
                            scores(g, w, k // 2)
                        elif cur and k == 4 and (w or not first):
                            outputs(*prev)
                        if nxt and k in MAXIMA[w]:
                            max_scores(n, maxima(w, nxt)[MAXIMA[w].index(k)])

            pe.wait_ge(ones_set, 1)
            transposes(0, 0, 0)
            for q in range(1, 3):
                pe.wait_ge(t_out, q)
                transposes(0, 0, q)
            groups(pe, body)
            outputs(GROUPS - 1, UNITS - 1)
            wait(pe, *freed(GROUPS - 1, ("D", 0, 0)))
            for k in range(DEN_STEPS):
                denominators(GROUPS - 1, 1, k)


def output_stage(nc, ot_dram, yx_dram, out, keep):
    ot_v = ot_dram.rearrange("(b g) f p q -> b f p g q", g=HG)
    yx_v = yx_dram.rearrange("(b p f i) d -> b f p i d", p=P, f=2, i=4)
    out_v = out.rearrange("b (p f i) d -> b f p i d", p=P, f=2, i=4)
    with ExitStack() as ctx:
        sb = lambda name, shape, dt=F32: ctx.enter_context(nc.sbuf_tensor(name, shape, dt))
        sem = lambda name: ctx.enter_context(nc.semaphore(name))
        ot = sb("attention_out", [P, 2, HG, BANK])
        oth = sb("attention_out_hi", [P, 2, HG, BANK], F32R)
        otl = sb("attention_out_lo", [P, 2, HG, BANK], F32R)
        wh = sb("woT_hi", [P, CD, D], F32R)
        wl = sb("woT_lo", [P, CD, D], F32R)
        y = sb("x_plus_ffn", [P, 2, 4, D])
        ps = ctx.enter_context(nc.psum_tensor("projected", [P, 4, BANK], F32))
        loaded = [sem("ot_loaded0"), sem("ot_loaded1")]
        y_loaded = [sem("y_loaded0"), sem("y_loaded1")]
        stored = [sem("out_stored0"), sem("out_stored1")]
        hi_ready, lo_ready, w_ready = sem("hi_ready"), sem("lo_ready"), sem("w_ready")
        full, summed = sem("projection_full"), sem("summed")
        block = ctx.enter_context(nc.Block())

        @block.sync
        def _(sp):
            def load(b, f):
                sp.dma_start(ot[:, f], ot_v[b][f]).then_inc(loaded[f], 16)
                sp.dma_start(y[:, f], yx_v[b][f]).then_inc(y_loaded[f], 16)

            load(0, 0)
            load(0, 1)
            with sp.Fori(1, B) as b:
                for f in range(2):
                    sp.wait_ge(summed, b * 8 + (4 * f - 4))
                    sp.dma_start(out_v[b - 1][f], y[:, f]).then_inc(stored[f], 16)
                    sp.dma_start(ot[:, f], ot_v[b][f]).then_inc(loaded[f], 16)
                    sp.wait_ge(stored[f], b * 16)
                    sp.dma_start(y[:, f], yx_v[b][f]).then_inc(y_loaded[f], 16)
            for f in range(2):
                sp.wait_ge(summed, 8 * B - 4 + 4 * f)
                sp.dma_start(out_v[B - 1][f], y[:, f]).then_inc(stored[f], 16)
            for f in range(2):
                sp.wait_ge(stored[f], 16 * B)

        @block.scalar
        def _(act):
            def body(b):
                for f in range(2):
                    act.wait_ge(loaded[f], lin(b, 16, 16))
                    wait(act, full, lin(b, 8, 4 * f - 4))
                    nc.scalar.copy(oth[:, f], ot[:, f]).then_inc(hi_ready, 1)

            nc.scalar.copy(wh[:], keep["woT"][:]).then_inc(w_ready, 1)
            body(0)
            with act.Fori(1, B) as b:
                body((b, 1, 0))

        @block.gpsimd
        def _(pool):
            def body(b):
                for f in range(2):
                    pool.wait_ge(hi_ready, lin(b, 2, f + 1))
                    nc.gpsimd.tensor_tensor(otl[:, f], ot[:, f], oth[:, f].bitcast(F32), ALU.subtract).then_inc(lo_ready, 1)

            body(0)
            with pool.Fori(1, B) as b:
                body((b, 1, 0))

        @block.tensor
        def _(pe):
            def body(b):
                for f in range(2):
                    pe.wait_ge(lo_ready, lin(b, 2, f + 1))
                    for i in range(4):
                        wait(pe, summed, lin(b, 8, 4 * f + i - 3))
                        terms = [(oo, ww, c) for c in range(CD) for oo, ww in ((oth, wh), (oth, wl), (otl, wh))]
                        for k, (oo, ww, c) in enumerate(terms):
                            last = nc.tensor.matmul(ps[:, i, :], oo[:, f, c, i * P:(i + 1) * P], ww[:, c, :],
                                                    start=(k == 0), stop=(k == len(terms) - 1))
                        last.then_inc(full, 1)

            pe.wait_ge(w_ready, 2)
            body(0)
            with pe.Fori(1, B) as b:
                body((b, 1, 0))

        @block.vector
        def _(dve):
            dve.wait_ge(w_ready, 1)
            nc.vector.tensor_tensor(wl[:], keep["woT"][:], wh[:].bitcast(F32), ALU.subtract).then_inc(w_ready, 1)
            with dve.Fori(0, B) as b:
                for f in range(2):
                    dve.wait_ge(y_loaded[f], b * 16 + 16)
                    for i in range(4):
                        dve.wait_ge(full, b * 8 + (4 * f + i + 1))
                        nc.vector.tensor_tensor(y[:, f, i, :], ps[:, i, :], y[:, f, i, :], ALU.add).then_inc(summed, 1)


def build(nc, x, W_qkv, W_o, w_fc, w_proj, out):
    qkv_dram = nc.dram_tensor("qkv_scratch", (B * L, E3), F32).ap()
    yx_dram = nc.dram_tensor("x_plus_ffn_scratch", (B * L, D), F32).ap()
    ot_dram = nc.dram_tensor("attention_scratch", (GROUPS, 2, P, BANK), F32).ap()
    den_dram = nc.dram_tensor("denominators_scratch", (2, 2, HG, BANK), F32).ap()
    with ExitStack() as ctx:
        sb = lambda name, shape, dt=F32: ctx.enter_context(nc.sbuf_tensor(name, shape, dt))
        keep = {
            "id32": sb("id32", [P, P]), "ones32": sb("ones32", [P, 32]), "powers": sb("powers_and_epsilons", [P, 12]),
            "woT": sb("woT", [P, CD, D]),
        }
        scalars = sb("scalars", [P, 8])
        names = ("scale", "unscale", "gamma1", "gamma2", "inv1", "ninv1", "gamma12")
        keep["scal"] = {k: scalars[:, j:j + 1] for j, k in enumerate(names)}
        with ExitStack() as weights:
            wsb = lambda name, shape, dt: weights.enter_context(nc.sbuf_tensor(name, shape, dt))
            keep["wh"] = wsb("wqkvT_hi", [P, CD, E3], F16)
            keep["wl"] = wsb("wqkvT_lo", [P, CD, E3], F16)
            keep["t1T"] = wsb("ternary_fcT", [P, CD, F], F16)
            keep["t2T"] = wsb("ternary_projT", [P, CF, D], F16)
            keep["colsum"] = wsb("ternary_proj_sums", [P, D], F32)
            weight_stage(nc, W_qkv, W_o, w_fc, w_proj, keep)
            token_stage(nc, x.rearrange("b l d -> (b l) d"), qkv_dram, yx_dram, keep)
        attention_stage(nc, qkv_dram, ot_dram, den_dram, keep)
        output_stage(nc, ot_dram, yx_dram, out, keep)


_INS = ["L0_attn_x", "L0_attn_W_qkv", "L0_attn_W_o", "L0_ffn_w_fc", "L0_ffn_w_proj"]


def kernel(**inputs):
    import numpy as np
    import concourse.bacc as bacc
    from concourse.bass_utils import run_bass_kernel_spmd

    nc = bacc.Bacc("TRN2", target_bir_lowering=False, num_devices=1)
    arrays, args = {}, []
    for name in _INS:
        a = np.ascontiguousarray(inputs[name])
        arrays[f"in_{name}"] = a
        args.append(nc.dram_tensor(f"in_{name}", a.shape, mybir.dt.from_np(a.dtype), kind="ExternalInput").ap())
    out = nc.dram_tensor("out_0", (B, L, D), F32, kind="ExternalOutput").ap()
    build(nc, *args, out)
    r = run_bass_kernel_spmd(nc, [arrays], core_ids=[0])
    return r.results[0]["out_0"]
```
